# Optimizing a Trainium2 kernel written in Bass

```python
import numpy as np
import jax
import jax.numpy as jnp

def _softmax(x, axis=-1):
    return jax.nn.softmax(x, axis=axis)

def _gelu(x):
    return jax.nn.gelu(x, approximate=True)

def _silu(x):
    return jax.nn.silu(x)

def _sigmoid(x):
    return jax.nn.sigmoid(x)

def _layernorm(x, axis=-1, eps=1e-05):
    m = jnp.mean(x, axis=axis, keepdims=True)
    v = jnp.var(x, axis=axis, keepdims=True)
    return (x - m) / jnp.sqrt(v + eps)

def _scatter_add(tgt, idx, src, axis=0):
    return tgt.at[idx].add(src)

def _segment_sum(src, seg, n):
    return jax.ops.segment_sum(src, seg, n)
kernel_name = 'mk_hybrid_d1_jaxref_r8_0e1078'

def setup_inputs(seed: int=0):
    np.random.seed(seed)
    _w = jnp.asarray

    def _L0_attn_a_setup():
        import jax, jax.numpy as jnp
        import numpy as np
        D = 128
        H = 16
        HD = D // H
        EPS = 1e-06

        def rms_norm(x, w):
            xf = x.astype(jnp.float32)
            rms = jnp.sqrt(jnp.mean(xf * xf, axis=-1, keepdims=True) + EPS)
            return (xf / rms * w.astype(jnp.float32)).astype(x.dtype)
        key = jax.random.key(seed)
        ks = jax.random.split(key, 6)
        B, S = (2, 256)
        x = jax.random.normal(ks[0], (B, S, D), dtype=jnp.float32)
        Wqkv = jax.random.normal(ks[1], (3 * D, D), dtype=jnp.float32) * (1.0 / np.sqrt(D))
        bqkv = jax.random.normal(ks[2], (3 * D,), dtype=jnp.float32) * 0.02
        Wproj = jax.random.normal(ks[3], (D, D), dtype=jnp.float32) * (1.0 / np.sqrt(D))
        bproj = jax.random.normal(ks[4], (D,), dtype=jnp.float32) * 0.02
        qn_w = jnp.ones((HD,), dtype=jnp.float32)
        kn_w = jnp.ones((HD,), dtype=jnp.float32)
        return {'x': x, 'Wqkv': Wqkv, 'bqkv': bqkv, 'Wproj': Wproj, 'bproj': bproj, 'qn_w': qn_w, 'kn_w': kn_w}
    _L0_attn_a_in = _L0_attn_a_setup()

    def _L0_attn_b_setup():
        import jax, jax.numpy as jnp
        import numpy as np
        import math
        B, T, E = (1, 256, 128)
        H = 8
        D = E // H // 2
        LAMBDA_INIT = 0.8 - 0.6 * math.exp(-0.3 * 1)
        SCALE_BASE = 512.0
        THETA = 10000.0

        def _rope_tables(T, d):
            inv_freq = 1.0 / THETA ** (jnp.arange(0, d, 2, dtype=jnp.float32) / d)
            pos = jnp.arange(T, dtype=jnp.float32)
            freqs = pos[:, None] * inv_freq[None, :]
            freqs = jnp.repeat(freqs, 2, axis=-1)
            sv = (jnp.arange(0, d, 2, dtype=jnp.float32) + 0.4 * d) / (1.4 * d)
            power = (pos - T // 2) / SCALE_BASE
            scale = sv[None, :] ** power[:, None]
            scale = jnp.concatenate([scale, scale], axis=-1)
            return (freqs, scale)

        def _rotate_half(x):
            x1 = x[..., 0::2]
            x2 = x[..., 1::2]
            return jnp.stack([-x2, x1], axis=-1).reshape(x.shape)

        def _apply_rope(t, freqs, scale):
            f = freqs[None, :, None, :]
            s = scale[None, :, None, :]
            return t * jnp.cos(f) * s + _rotate_half(t) * jnp.sin(f) * s
        key = jax.random.key(seed)
        ks = jax.random.split(key, 9)
        w = 0.02
        return {'x': jax.random.normal(ks[0], (B, T, E), dtype=jnp.float32), 'Wq': jax.random.normal(ks[1], (E, E), dtype=jnp.float32) * w, 'Wk': jax.random.normal(ks[2], (E, E), dtype=jnp.float32) * w, 'Wv': jax.random.normal(ks[3], (E, E), dtype=jnp.float32) * w, 'Wo': jax.random.normal(ks[4], (E, E), dtype=jnp.float32) * w, 'lambda_q1': jax.random.normal(ks[5], (D,), dtype=jnp.float32) * 0.1, 'lambda_k1': jax.random.normal(ks[6], (D,), dtype=jnp.float32) * 0.1, 'lambda_q2': jax.random.normal(ks[7], (D,), dtype=jnp.float32) * 0.1, 'lambda_k2': jax.random.normal(ks[8], (D,), dtype=jnp.float32) * 0.1}
    _L0_attn_b_in = _L0_attn_b_setup()

    def _L0_ffn_setup():
        import jax, jax.numpy as jnp
        import numpy as np
        DIM = 128
        HIDDEN = 128
        NUM_EXPERTS = 8
        TOP_K = 2
        key = jax.random.key(seed)
        ks = jax.random.split(key, 8)
        std = 0.02
        x = jax.random.normal(ks[0], (2, 128, DIM), dtype=jnp.float32)
        gate_w = jax.random.normal(ks[1], (NUM_EXPERTS, DIM), dtype=jnp.float32) * std
        w1 = jax.random.normal(ks[2], (NUM_EXPERTS, DIM, HIDDEN), dtype=jnp.float32) * std
        w2 = jax.random.normal(ks[3], (NUM_EXPERTS, HIDDEN, DIM), dtype=jnp.float32) * std
        w3 = jax.random.normal(ks[4], (NUM_EXPERTS, DIM, HIDDEN), dtype=jnp.float32) * std
        w1s = jax.random.normal(ks[5], (1, DIM, HIDDEN), dtype=jnp.float32) * std
        w2s = jax.random.normal(ks[6], (1, HIDDEN, DIM), dtype=jnp.float32) * std
        w3s = jax.random.normal(ks[7], (1, DIM, HIDDEN), dtype=jnp.float32) * std
        return {'x': x, 'gate_w': gate_w, 'w1': w1, 'w2': w2, 'w3': w3, 'w1s': w1s, 'w2s': w2s, 'w3s': w3s}
    _L0_ffn_in = _L0_ffn_setup()
    _d = {'L0_attn_a_x': _L0_attn_a_in['x'], 'L0_attn_a_Wqkv': _L0_attn_a_in['Wqkv'], 'L0_attn_a_bqkv': _L0_attn_a_in['bqkv'], 'L0_attn_a_Wproj': _L0_attn_a_in['Wproj'], 'L0_attn_a_bproj': _L0_attn_a_in['bproj'], 'L0_attn_a_qn_w': _L0_attn_a_in['qn_w'], 'L0_attn_a_kn_w': _L0_attn_a_in['kn_w'], 'L0_attn_b_Wq': _L0_attn_b_in['Wq'], 'L0_attn_b_Wk': _L0_attn_b_in['Wk'], 'L0_attn_b_Wv': _L0_attn_b_in['Wv'], 'L0_attn_b_Wo': _L0_attn_b_in['Wo'], 'L0_attn_b_lambda_q1': _L0_attn_b_in['lambda_q1'], 'L0_attn_b_lambda_k1': _L0_attn_b_in['lambda_k1'], 'L0_attn_b_lambda_q2': _L0_attn_b_in['lambda_q2'], 'L0_attn_b_lambda_k2': _L0_attn_b_in['lambda_k2'], 'L0_ffn_gate_w': _L0_ffn_in['gate_w'], 'L0_ffn_w1': _L0_ffn_in['w1'], 'L0_ffn_w2': _L0_ffn_in['w2'], 'L0_ffn_w3': _L0_ffn_in['w3'], 'L0_ffn_w1s': _L0_ffn_in['w1s'], 'L0_ffn_w2s': _L0_ffn_in['w2s'], 'L0_ffn_w3s': _L0_ffn_in['w3s']}
    _x0 = _d['L0_attn_a_x']
    _d['L0_attn_a_x'] = jax.random.normal(jax.random.fold_in(jax.random.key(seed), 1), (16, 256, 128), dtype=_x0.dtype)
    del _x0
    return _d

def reference(L0_attn_a_x, L0_attn_a_Wqkv, L0_attn_a_bqkv, L0_attn_a_Wproj, L0_attn_a_bproj, L0_attn_a_qn_w, L0_attn_a_kn_w, L0_attn_b_Wq, L0_attn_b_Wk, L0_attn_b_Wv, L0_attn_b_Wo, L0_attn_b_lambda_q1, L0_attn_b_lambda_k1, L0_attn_b_lambda_q2, L0_attn_b_lambda_k2, L0_ffn_gate_w, L0_ffn_w1, L0_ffn_w2, L0_ffn_w3, L0_ffn_w1s, L0_ffn_w2s, L0_ffn_w3s):

    def _L0_attn_a_ref(x, Wqkv, bqkv, Wproj, bproj, qn_w, kn_w):
        import jax, jax.numpy as jnp
        import numpy as np
        D = 128
        H = 16
        HD = D // H
        EPS = 1e-06

        def rms_norm(x, w):
            xf = x.astype(jnp.float32)
            rms = jnp.sqrt(jnp.mean(xf * xf, axis=-1, keepdims=True) + EPS)
            return (xf / rms * w.astype(jnp.float32)).astype(x.dtype)
        B, S, _ = x.shape
        qkv = x @ Wqkv.T + bqkv
        qkv = qkv.reshape(B, S, 3, H, HD)
        q, k, v = (qkv[:, :, 0], qkv[:, :, 1], qkv[:, :, 2])
        q = rms_norm(q, qn_w)
        k = rms_norm(k, kn_w)
        q = q.transpose(0, 2, 1, 3)
        k = k.transpose(0, 2, 1, 3)
        v = v.transpose(0, 2, 1, 3)
        scale = 1.0 / np.sqrt(HD)
        scores = jnp.einsum('bhsd,bhtd->bhst', q, k) * scale
        attn = jax.nn.softmax(scores, axis=-1)
        out = jnp.einsum('bhst,bhtd->bhsd', attn, v)
        out = out.transpose(0, 2, 1, 3).reshape(B, S, D)
        return out @ Wproj.T + bproj

    def _L0_attn_b_ref(x, Wq, Wk, Wv, Wo, lambda_q1, lambda_k1, lambda_q2, lambda_k2):
        import jax, jax.numpy as jnp
        import numpy as np
        import math
        B, T, E = (1, 256, 128)
        H = 8
        D = E // H // 2
        LAMBDA_INIT = 0.8 - 0.6 * math.exp(-0.3 * 1)
        SCALE_BASE = 512.0
        THETA = 10000.0

        def _rope_tables(T, d):
            inv_freq = 1.0 / THETA ** (jnp.arange(0, d, 2, dtype=jnp.float32) / d)
            pos = jnp.arange(T, dtype=jnp.float32)
            freqs = pos[:, None] * inv_freq[None, :]
            freqs = jnp.repeat(freqs, 2, axis=-1)
            sv = (jnp.arange(0, d, 2, dtype=jnp.float32) + 0.4 * d) / (1.4 * d)
            power = (pos - T // 2) / SCALE_BASE
            scale = sv[None, :] ** power[:, None]
            scale = jnp.concatenate([scale, scale], axis=-1)
            return (freqs, scale)

        def _rotate_half(x):
            x1 = x[..., 0::2]
            x2 = x[..., 1::2]
            return jnp.stack([-x2, x1], axis=-1).reshape(x.shape)

        def _apply_rope(t, freqs, scale):
            f = freqs[None, :, None, :]
            s = scale[None, :, None, :]
            return t * jnp.cos(f) * s + _rotate_half(t) * jnp.sin(f) * s
        b, t, e = x.shape
        scaling = D ** (-0.5)
        q = (x @ Wq.T).reshape(b, t, 2 * H, D)
        k = (x @ Wk.T).reshape(b, t, 2 * H, D)
        v = (x @ Wv.T).reshape(b, t, H, 2 * D)
        freqs, scale = _rope_tables(t, D)
        q = _apply_rope(q, freqs, scale)
        k = _apply_rope(k, freqs, 1.0 / scale)
        q = jnp.transpose(q, (0, 2, 1, 3)) * scaling
        k = jnp.transpose(k, (0, 2, 1, 3))
        v = jnp.transpose(v, (0, 2, 1, 3))
        scores = jnp.einsum('bhtd,bhsd->bhts', q, k)
        probs = jax.nn.softmax(scores.astype(jnp.float32), axis=-1).astype(scores.dtype)
        lam1 = jnp.exp(jnp.sum(lambda_q1 * lambda_k1))
        lam2 = jnp.exp(jnp.sum(lambda_q2 * lambda_k2))
        lam = lam1 - lam2 + LAMBDA_INIT
        probs = probs.reshape(b, H, 2, t, t)
        diff = probs[:, :, 0] - lam * probs[:, :, 1]
        attn = jnp.einsum('bhts,bhsd->bhtd', diff, v)
        attn = attn * jax.lax.rsqrt(jnp.mean(attn * attn, axis=-1, keepdims=True) + 1e-05)
        attn = attn * (1.0 - LAMBDA_INIT)
        attn = jnp.transpose(attn, (0, 2, 1, 3)).reshape(b, t, e)
        return attn @ Wo.T

    def _L0_ffn_ref(x, gate_w, w1, w2, w3, w1s, w2s, w3s):
        import jax, jax.numpy as jnp
        import numpy as np
        DIM = 128
        HIDDEN = 128
        NUM_EXPERTS = 8
        TOP_K = 2
        bs, slen, dim = x.shape
        xt = x.reshape(bs * slen, dim)
        logits = xt @ gate_w.T
        scores = jax.nn.softmax(logits.astype(jnp.float32), axis=1).astype(x.dtype)
        top_scores, sel = jax.lax.top_k(scores, TOP_K)
        sel_flat = sel.reshape(-1)
        order = jnp.argsort(sel_flat, stable=True)
        top_scores_sorted = top_scores.reshape(-1)[order]
        token_idx = order // TOP_K
        eid = sel_flat[order]
        routed_in = xt[token_idx] * top_scores_sorted[:, None]
        out_routed = jnp.zeros_like(routed_in)
        for e in range(NUM_EXPERTS):
            m = (eid == e)[:, None]
            xe = jnp.where(m, routed_in, 0.0)
            h = jax.nn.silu(xe @ w1[e]) * (xe @ w3[e])
            out_routed = out_routed + jnp.where(m, h @ w2[e], 0.0)
        hs = jax.nn.silu(xt @ w1s[0]) * (xt @ w3s[0])
        out = hs @ w2s[0]
        out = out.at[token_idx].add(out_routed)
        return out.reshape(bs, slen, dim)
    x = L0_attn_a_x
    x = x + _L0_attn_a_ref(_layernorm(x, axis=-1), L0_attn_a_Wqkv, L0_attn_a_bqkv, L0_attn_a_Wproj, L0_attn_a_bproj, L0_attn_a_qn_w, L0_attn_a_kn_w)
    x = x + _L0_ffn_ref(_layernorm(x, axis=-1), L0_ffn_gate_w, L0_ffn_w1, L0_ffn_w2, L0_ffn_w3, L0_ffn_w1s, L0_ffn_w2s, L0_ffn_w3s)
    x = x + _L0_attn_b_ref(_layernorm(x, axis=-1), L0_attn_b_Wq, L0_attn_b_Wk, L0_attn_b_Wv, L0_attn_b_Wo, L0_attn_b_lambda_q1, L0_attn_b_lambda_k1, L0_attn_b_lambda_q2, L0_attn_b_lambda_k2)
    x = x + _L0_ffn_ref(_layernorm(x, axis=-1), L0_ffn_gate_w, L0_ffn_w1, L0_ffn_w2, L0_ffn_w3, L0_ffn_w1s, L0_ffn_w2s, L0_ffn_w3s)
    return x

_drawn_inputs = setup_inputs


def setup_inputs(seed=0):
    import zlib

    import numpy as np

    out = dict(_drawn_inputs(seed))
    spreads = {'L0_attn_a_qn_w': (1.0, 0.2), 'L0_attn_a_kn_w': (1.0, 0.2)}
    factors = {'L0_attn_b_Wq': 4.538,
     'L0_attn_b_Wk': 4.399,
     'L0_attn_b_lambda_q1': 8.0,
     'L0_attn_b_lambda_k1': 8.0,
     'L0_attn_b_lambda_q2': 8.0,
     'L0_attn_b_lambda_k2': 8.0,
     'L0_ffn_gate_w': 8.0,
     'L0_ffn_w1': 8.0,
     'L0_ffn_w2': 8.0,
     'L0_ffn_w3': 8.0,
     'L0_ffn_w1s': 5.003,
     'L0_ffn_w2s': 4.973,
     'L0_ffn_w3s': 4.906}
    for name, (base, spread) in spreads.items():
        noise = np.random.default_rng([zlib.crc32(name.encode()), seed]).standard_normal(out[name].shape)
        drawn = base * np.exp(spread * noise) if base else spread * noise
        out[name] = jnp.asarray(drawn.astype(out[name].dtype))
    for name, factor in factors.items():
        out[name] = (out[name] * factor).astype(out[name].dtype)
    return out
```

```python
from contextlib import ExitStack

import numpy as np

import concourse.bass as bass
from concourse import mybir

F32 = mybir.dt.float32
F32R = mybir.dt.float32r
I32 = mybir.dt.int32
U32 = mybir.dt.uint32
ALU = mybir.AluOpType
ACT = mybir.ActivationFunctionType
AX = mybir.AxisListType

P = 128
NSEQ, SEQ, DIM = 16, 256, 128
NT = NSEQ * SEQ // P
HEADS = 16
HD = 8
LN_EPS = 1e-5
RMS_EPS_A = 1e-6
RMS_EPS_B = 1e-5
SCALE = 1.0 / float(np.sqrt(HD))
LAMBDA_INIT = 0.8 - 0.6 * float(np.exp(-0.3))
E = 8
NCH, CH = 8, 512
PAIRS = HEADS // 2
UNITS = 16
UNITS_AT = {3: 3, 4: 4, 5: 4, 6: 3, 7: 2}


class Events:

    def __init__(self, ctx, nc, name, per):
        self.make = lambda: ctx.enter_context(nc.semaphore(name))
        self.taken = None
        self.per = per

    @property
    def sem(self):
        if self.taken is None:
            self.taken = self.make()
        return self.taken

    def upto(self, n, j=None):
        value = (n * self.per + (self.per if j is None else j)).at
        return max(value, 0) if isinstance(value, int) else value


class Step:

    def __init__(self, register, turns, offset):
        self.register, self.turns, self.offset = register, turns, offset

    def __add__(self, x):
        return Step(self.register, self.turns, self.offset + x)

    def __sub__(self, x):
        return self + -x

    def __mul__(self, x):
        return Step(self.register, self.turns * x, self.offset * x)

    @property
    def at(self):
        if self.register is None:
            return self.offset
        return self.register * self.turns + self.offset if self.offset else self.register * self.turns


class Shared:
    pass


def bc(ap, shape):
    return ap.broadcast_to(shape)


def setup(nc, ctx, g, d):
    loads = [
        (g.identity[:], d["identity"]),
        (g.x[:, :, :], d["x"].rearrange("b (c p) d -> p (b c) d", p=P)),
        (g.wqkv_a[:], d["Wqkv_aT"]),
        (g.bqkv[:], d["bqkv"].partition_broadcast(P)),
        (g.qk_w[:, 0, :], d["qn_w"].partition_broadcast(P)),
        (g.qk_w[:, 1, :], d["kn_w"].partition_broadcast(P)),
        (g.wproj[:], d["WprojT"]),
        (g.bproj[:], d["bproj"].partition_broadcast(P)),
        (g.select_raw[:], d["select"]),
        (g.iota[:], d["iota"]),
        (g.gate[:], d["gate_wT"]),
        (g.w1[:, 0:E, :], d["w1"].rearrange("e p n -> p e n")),
        (g.w3[:, 0:E, :], d["w3"].rearrange("e p n -> p e n")),
        (g.w2[:, 0:E, :], d["w2"].rearrange("e p n -> p e n")),
        (g.w1[:, E, :], d["w1s"][0]),
        (g.w3[:, E, :], d["w3s"][0]),
        (g.w2[:, E, :], d["w2s"][0]),
        (g.wqkv_b[:], d["Wqkv_bT"]),
        (g.wo[:], d["WoT"]),
        (g.rope_cos[:], d["rope_cos"]),
        (g.rope_sin[:], d["rope_sin"]),
        (g.lam_in[:, 0, :], d["lambda_q1"].partition_broadcast(P)),
        (g.lam_in[:, 1, :], d["lambda_q2"].partition_broadcast(P)),
        (g.lam_in[:, 2, :], d["lambda_k1"].partition_broadcast(P)),
        (g.lam_in[:, 3, :], d["lambda_k2"].partition_broadcast(P)),
    ]
    loaded = ctx.enter_context(nc.semaphore("setup_loaded"))
    dve_step = ctx.enter_context(nc.semaphore("setup_dve_step"))
    var_ready = ctx.enter_context(nc.semaphore("setup_var_ready"))
    dev_ready = ctx.enter_context(nc.semaphore("setup_dev_ready"))
    dots_ready = ctx.enter_context(nc.semaphore("setup_dots_ready"))
    lam_ready = ctx.enter_context(nc.semaphore("setup_lam_ready"))
    stat = ctx.enter_context(nc.sbuf_tensor("setup_stat", [P, NT, 6], F32))
    mv = ctx.enter_context(nc.sbuf_tensor("setup_mv", [P, NT, 2], F32))
    tiny = ctx.enter_context(nc.sbuf_tensor("setup_tiny", [P, 64], F32))
    with nc.Block() as block:

        @block.sync
        def _(sp):
            for out, in_ in loads:
                sp.dma_start(out, in_).then_inc(loaded, 16)

        @block.gpsimd
        def _(pool):
            pool.memset(g.minus_half[:], -0.5)
            pool.memset(g.three_halves[:], 1.5)
            pool.memset(g.euler[:], float(np.e))
            pool.memset(g.ln_eps[:], LN_EPS)

        @block.scalar
        def _(act):
            act.wait_ge(var_ready, 1)
            act.activation(g.rstd[0][:], g.rstd[0][:], ACT.Sqrt).then_inc(dev_ready, 1)
            act.wait_ge(dots_ready, 1)
            act.activation(tiny[:, 2:4], tiny[:, 0:2], ACT.Exp).then_inc(lam_ready, 1)

        @block.vector
        def _(dve):
            count = [0]

            def step(ins):
                count[0] += 1
                ins.then_inc(dve_step, 1)
                dve.wait_ge(dve_step, count[0])

            dve.wait_ge(loaded, 16 * len(loads))
            for t in range(NT):
                ins = dve.bn_stats(stat[:, t, :], g.x[:, t, :])
            step(ins)
            for t in range(NT):
                ins = dve.bn_aggr(mv[:, t, :], stat[:, t, :])
            step(ins)
            dve.tensor_copy(g.mean[0][:], mv[:, :, 0])
            dve.tensor_scalar(g.rstd[0][:], mv[:, :, 1], LN_EPS, None, ALU.add).then_inc(var_ready, 1)
            dve.wait_ge(dev_ready, 1)
            step(dve.reciprocal(g.rstd[0][:], g.rstd[0][:]))
            step(dve.tensor_tensor(tiny[:, 8:16], g.qk_w[:, 0, :], g.qk_w[:, 1, :], ALU.mult))
            step(dve.tensor_scalar(g.qk_scale[:].rearrange("p (h d) -> p h d", d=HD),
                                   bc(tiny[:, 8:16].unsqueeze(1), [P, HEADS, HD]), SCALE, None, ALU.mult))
            step(dve.tensor_reduce(tiny[:, 16:17], tiny[:, 8:16], AX.X, ALU.max, apply_absolute_value=True))
            step(dve.tensor_scalar(g.minus_bound[:], tiny[:, 16:17], -HD * SCALE, None, ALU.mult))
            step(dve.tensor_tensor(tiny[:, 24:40].rearrange("p (a b) -> p a b", a=2),
                                   g.lam_in[:, 0:2, :], g.lam_in[:, 2:4, :], ALU.mult))
            dve.tensor_reduce(tiny[:, 0:2], tiny[:, 24:40].rearrange("p (a b) -> p a b", a=2),
                              AX.X, ALU.add).then_inc(dots_ready, 1)
            dve.wait_ge(lam_ready, 1)
            step(dve.tensor_tensor(tiny[:, 4:5], tiny[:, 3:4], tiny[:, 2:3], ALU.subtract))
            step(dve.tensor_scalar(g.minus_lam[:], tiny[:, 4:5], -LAMBDA_INIT, None, ALU.add))
            step(dve.tensor_copy(g.select[:], g.select_raw[:]))


def attention(nc, ctx, g, tag, psum):
    a, b = tag == "a", tag == "b"
    VW = 8 if a else 16
    mean, rstd = (g.mean[0], g.rstd[0]) if a else (g.mean[2], g.rstd[2])
    mean_next, rstd_next = (g.mean[1], g.rstd[1]) if a else (g.mean[3], g.rstd[3])
    wqkv, wout = (g.wqkv_a, g.wproj) if a else (g.wqkv_b, g.wo)
    X2 = g.x[:, :, :].rearrange("p (n c) d -> p n (c d)", c=2)

    def sb(name, shape, dt=F32):
        return ctx.enter_context(nc.sbuf_tensor(f"{tag}_{name}", shape, dt))

    def ev(name, per):
        return Events(ctx, nc, f"{tag}_{name}", per)

    xn, xt = g.s_xn, g.s_xt
    qkv, qh = g.s_qkv, g.s_qh
    qs, ks, v1 = g.s_qs, g.s_ks, g.s_v1
    kt, qt, qp = g.s_kt, g.s_qt, g.s_qp
    probs, ot, an, at = g.s_probs, g.s_ot, g.s_an, g.s_at
    sq, ss, vh, y, yt = g.s_sq, g.s_ss, g.s_vh, g.s_y, g.s_yt
    rs, tv, a2 = g.s_rs, g.s_tv, g.s_a2
    S = psum[:, 0:2048]
    PV = psum[:, 2048:2304]
    M = [psum[:, 2560:3072], psum[:, 3072:3584]]
    T = psum[:, 3584:4096]
    if a:
        bank = {"kt": M[0], "qp": M[0], "xt": T, "qkv": T, "otr": M[1], "atr": M[1], "pj": M[1]}
    else:
        bank = {x: T for x in ("kt", "qp", "xt", "qkv", "otr", "atr", "pj", "qf")}

    filled = ev("filled", 1)
    xn_sb, xt_mm, xt_sb = ev("xn_sb", 2), ev("xt_mm", 1), ev("xt_sb", 1)
    xb_sb = ev("xb_sb", 1)
    qkv_mm, qkv_sb, v_sb = ev("qkv_mm", 2), ev("qkv_sb", 2), ev("v_sb", 1)
    sq_sb, ss_sb, seed, newton, inv_sb = ev("sq_sb", 1), ev("ss_sb", 1), ev("seed", 4), ev("newton", 12), ev("inv_sb", 1)
    rot, qh_sb, hi_sb, lo_sb = ev("rot", 2), ev("qh_sb", 2 if a else 1), ev("hi_sb", 2), ev("lo_sb", 2)
    kt_mm, kt_sb, qp_mm, qp_sb = ev("kt_mm", 2), ev("kt_sb", 2), ev("qp_mm", 2), ev("qp_sb", 2)
    mx_mm, mx_sb, qf_mm, qf_sb = ev("mx_mm", UNITS), ev("mx_sb", UNITS), ev("qf_mm", 2), ev("qf_sb", 2)
    s_mm, ex_sb, pv_mm, ot_sb = ev("s_mm", PAIRS), ev("ex_sb", PAIRS), ev("pv_mm", PAIRS), ev("ot_sb", 4)
    otr_mm, otr_used = ev("otr_mm", 2), ev("otr_used", 2)
    rs_sb, tv_sb, a2_sb = ev("rs_sb", 4), ev("tv_sb", 2), ev("a2_sb", 2)
    sq2_sb, ms_sb, var_sb, inv2_sb = ev("sq2_sb", 1), ev("ms_sb", 1), ev("var_sb", 1), ev("inv2_sb", 1)
    an_sb, atr_mm, at_sb, pj_mm, x_sb = ev("an_sb", 2), ev("atr_mm", 1), ev("at_sb", 1), ev("pj_mm", 1), ev("x_sb", 1)
    bn_sb, mv_sb, vare_sb, rstd_sb = ev("bn_sb", 1), ev("mv_sb", 1), ev("vare_sb", 1), ev("rstd_sb", 1)
    q_ready = qp_sb if a else qf_sb

    def march(eng, body):
        for n in (-2, -1, 0, 1):
            body(Step(None, 0, n), n)
        with eng.Fori(0, 6) as i:
            body(Step(i, 2, 2), 2)
            body(Step(i, 2, 3), 3)
        for n in (14, 15, 16):
            body(Step(None, 0, n), n)

    def doing(k):
        return k + 2 < NSEQ, 0 <= k + 1 < NSEQ, 0 <= k < NSEQ, 0 <= k - 1 < NSEQ

    with nc.Block() as block:

        @block.tensor
        def _(pe):
            def turn(dst, src):
                for q in range(4):
                    ins = pe.transpose(dst[:, q * P:(q + 1) * P], src[:, q * P:(q + 1) * P], g.identity[:])
                return ins

            def body(n, k):
                one, two, att, out = doing(k)
                before = 0 <= k - 1 < NSEQ

                def scores(p):
                    if p == 0:
                        pe.wait_ge(kt_sb.sem, kt_sb.upto(n))
                        pe.wait_ge(q_ready.sem, q_ready.upto(n))
                    pe.wait_ge(ex_sb.sem, ex_sb.upto(n, p - 1))
                    for c in range(2):
                        for j in range(2):
                            h = 2 * p + j
                            q, r = h // 4, 32 * (h % 4)
                            o = (2 * (p % 2) + j) * 512 + c * SEQ
                            ins = pe.matmul(S[:, o:o + SEQ], kt[r:r + 32, k % 2, q, c * P:(c + 1) * P],
                                            qt[r:r + 32, k % 2, q, :], start=True, stop=True)
                    ins.then_inc(s_mm.sem, 1)

                def values(m, km, p):
                    if p == 0:
                        pe.wait_ge(v_sb.sem, v_sb.upto(m))
                    pe.wait_ge(ex_sb.sem, ex_sb.upto(m, p + 1))
                    if p % 2 == 0:
                        pe.wait_ge(ot_sb.sem, ot_sb.upto(m, p // 2))
                    for c in range(2):
                        for j in range(2):
                            h = 2 * p + j
                            r = 32 * (h % 4)
                            w = v1[:, km % 2, c, h if a else h // 2, :]
                            ins = pe.matmul(PV[r:r + 32, :], w, probs[:, p % 4, j, c, :],
                                            start=(c == 0), stop=(c == 1))
                    ins.then_inc(pv_mm.sem, 1)

                def k_turn(c):
                    if c == 0:
                        pe.wait_ge(lo_sb.sem, lo_sb.upto(n + 1))
                        pe.wait_ge((qp_sb if a else qf_sb).sem, (qp_sb if a else qf_sb).upto(n))
                    else:
                        pe.wait_ge(kt_sb.sem, kt_sb.upto(n + 1, 1))
                    turn(bank["kt"], ks[:, (k + 1) % 2, c]).then_inc(kt_mm.sem, 1)

                def q_turn(c):
                    if a:
                        pe.wait_ge(kt_sb.sem, kt_sb.upto(n + 1))
                        pe.wait_ge(qp_sb.sem, qp_sb.upto(n + 1, c))
                    elif c == 0:
                        pe.wait_ge(kt_sb.sem, kt_sb.upto(n + 1))
                        if one:
                            pe.wait_ge(xt_sb.sem, xt_sb.upto(n + 2))
                        pe.wait_ge(otr_used.sem, otr_used.upto(n - 1, 1))
                    else:
                        pe.wait_ge(qp_sb.sem, qp_sb.upto(n + 1, 1))
                        pe.wait_ge(otr_used.sem, otr_used.upto(n - 1))
                        if one:
                            pe.wait_ge(qkv_sb.sem, qkv_sb.upto(n + 2, 1))
                    turn(bank["qp"], qs[:, (k + 1) % 2, c]).then_inc(qp_mm.sem, 1)

                def q_final(c):
                    pe.wait_ge(mx_sb.sem, mx_sb.upto(n + 1, 8 * c + 8))
                    pe.wait_ge(x_sb.sem, x_sb.upto(n - 1))
                    if one:
                        pe.wait_ge(qkv_sb.sem, qkv_sb.upto(n + 2))
                    pe.wait_ge(qf_sb.sem, qf_sb.upto(n + 1, c))
                    turn(bank["qf"], qs[:, (k + 1) % 2, c]).then_inc(qf_mm.sem, 1)

                def maxima(u):
                    c, v = u // 8, u % 8
                    r, pair = 32 * (v % 4), v // 4
                    if u == 0:
                        pe.wait_ge(kt_sb.sem, kt_sb.upto(n + 1))
                        pe.wait_ge(qp_sb.sem, qp_sb.upto(n + 1, 1))
                    if u == 8:
                        pe.wait_ge(qp_sb.sem, qp_sb.upto(n + 1, 2))
                    pe.wait_ge(mx_sb.sem, mx_sb.upto(n + 1, u - 1))
                    for j in range(2):
                        q = 2 * pair + j
                        ins = pe.matmul(M[u % 2][:, j * SEQ:(j + 1) * SEQ], qp[r:r + 24, q, c * P:(c + 1) * P],
                                        kt[r:r + 24, (k + 1) % 2, q, :], start=True, stop=True)
                    ins.then_inc(mx_mm.sem, 1)

                def x_turn():
                    pe.wait_ge(xn_sb.sem, xn_sb.upto(n + 2))
                    if a:
                        pe.wait_ge(qkv_sb.sem, qkv_sb.upto(n + 1))
                    else:
                        pe.wait_ge(kt_sb.sem, kt_sb.upto(n + 1))
                    for c in range(2):
                        ins = pe.transpose(bank["xt"][:, c * P:(c + 1) * P], xn[:, c, :], g.identity[:])
                    ins.then_inc(xt_mm.sem, 1)

                def project(c):
                    if c == 0:
                        pe.wait_ge(xt_sb.sem, xt_sb.upto(n + 2))
                    pe.wait_ge(qkv_sb.sem, qkv_sb.upto(n + 2, c))
                    if b:
                        pe.wait_ge(otr_used.sem, otr_used.upto(n - 1))
                        if two:
                            pe.wait_ge(qp_sb.sem, qp_sb.upto(n + 1, c + 1))
                    pe.matmul(bank["qkv"][:, 0:3 * P], xt[:, c * P:(c + 1) * P], wqkv[:],
                                          start=True, stop=True).then_inc(qkv_mm.sem, 1)

                def o_turn(c):
                    if c == 0:
                        pe.wait_ge(ot_sb.sem, ot_sb.upto(n - 1))
                    pe.wait_ge(x_sb.sem, x_sb.upto(n - 2))
                    pe.wait_ge(otr_used.sem, otr_used.upto(n - 1, c))
                    if b and one and c == 0:
                        pe.wait_ge(xt_sb.sem, xt_sb.upto(n + 2))
                    if b and two:
                        pe.wait_ge(kt_sb.sem, kt_sb.upto(n + 1))
                        pe.wait_ge(qp_sb.sem, qp_sb.upto(n + 1, c))
                    for q in range(4):
                        ins = pe.transpose(bank["otr"][:, q * P:(q + 1) * P], ot[:, q, c * P:(c + 1) * P], g.identity[:])
                    ins.then_inc(otr_mm.sem, 1)

                def a_turn():
                    pe.wait_ge(an_sb.sem, an_sb.upto(n - 1))
                    if b and one:
                        pe.wait_ge(qkv_sb.sem, qkv_sb.upto(n + 2))
                    if b and two:
                        pe.wait_ge(qp_sb.sem, qp_sb.upto(n + 1))
                    for c in range(2):
                        ins = pe.transpose(bank["atr"][:, c * P:(c + 1) * P], an[:, c, :], g.identity[:])
                    ins.then_inc(atr_mm.sem, 1)

                def out_project():
                    pe.wait_ge(at_sb.sem, at_sb.upto(n - 1))
                    for c in range(2):
                        ins = pe.matmul(bank["pj"][:, c * P:(c + 1) * P], at[:, c * P:(c + 1) * P], wout[:],
                                        start=True, stop=True)
                    ins.then_inc(pj_mm.sem, 1)

                for p in range(PAIRS):
                    if att:
                        scores(p)
                    if a:
                        if two and p in (2, 3):
                            k_turn(p - 2)
                        if two and p in (4, 5):
                            q_turn(p - 4)
                        if out and p in (2, 3):
                            o_turn(p - 2)
                    else:
                        if two and p in (0, 1):
                            k_turn(p)
                        if out and p in (2, 3):
                            o_turn(p - 2)
                        if two and p == 4:
                            q_turn(1)
                    if p >= 2 and att:
                        values(n, k, p - 2)
                    if p < 2 and before:
                        values(n - 1, k - 1, p + 6)
                    if one and p == 1:
                        x_turn()
                    if a:
                        if one and p in (2, 3):
                            project(p - 2)
                    else:
                        if two and p == 2:
                            q_turn(0)
                        if one and p in (3, 4):
                            project(p - 3)
                    if out and p == 6:
                        a_turn()
                    if out and p == 7:
                        out_project()
                    if b and two:
                        if p == 7:
                            q_final(0)
                        for u in range(UNITS):
                            if sum(UNITS_AT.get(z, 0) for z in range(p)) <= u < sum(
                                    UNITS_AT.get(z, 0) for z in range(p + 1)):
                                maxima(u)
                        if p == 7:
                            q_final(1)

            march(pe, body)

        @block.scalar
        def _(act):
            def copy(out, in_):
                return act.activation(out, in_, ACT.Copy)

            def body(n, k):
                one, two, att, out = doing(k)
                before = 0 <= k - 1 < NSEQ

                def four(ap):
                    return ap.rearrange("p (q t) -> p q t", q=4)

                def k_keep(c):
                    act.wait_ge(kt_mm.sem, kt_mm.upto(n + 1, c + 1))
                    copy(kt[:, (k + 1) % 2, :, c * P:(c + 1) * P], four(bank["kt"])).then_inc(kt_sb.sem, 1)

                def q_keep(c):
                    act.wait_ge(qp_mm.sem, qp_mm.upto(n + 1, c + 1))
                    if b:
                        act.wait_ge(mx_mm.sem, mx_mm.upto(n))
                    copy(qp[:, :, c * P:(c + 1) * P], four(bank["qp"])).then_inc(qp_sb.sem, 1)

                def q_final_keep(c):
                    act.wait_ge(qf_mm.sem, qf_mm.upto(n + 1, c + 1))
                    copy(qt[:, (k + 1) % 2, :, c * P:(c + 1) * P], four(bank["qf"])).then_inc(qf_sb.sem, 1)

                def o_keep(m, q):
                    act.wait_ge(pv_mm.sem, pv_mm.upto(m, 2 * q + 2))
                    if q == 0:
                        act.wait_ge(otr_mm.sem, otr_mm.upto(m - 1))
                    copy(ot[:, q, :], PV).then_inc(ot_sb.sem, 1)

                for p in range(PAIRS):
                    if att:
                        act.wait_ge(s_mm.sem, s_mm.upto(n, p + 1))
                        if p >= 4:
                            act.wait_ge(pv_mm.sem, pv_mm.upto(n, p - 3))
                        else:
                            act.wait_ge(pv_mm.sem, pv_mm.upto(n - 1, p + 5))
                        dst = probs[:, p % 4, :, :, :].rearrange("p j c s -> p (j c s)")
                        act.activation(dst, S[:, (p % 2) * 1024:(p % 2 + 1) * 1024], ACT.Exp,
                                                  bias=g.minus_bound[:] if a else 0.0).then_inc(ex_sb.sem, 1)
                    if a and two and p in (2, 3):
                        k_keep(p - 2)
                    if b:
                        if two and p in (0, 1):
                            k_keep(p)
                        if p == 1 and before:
                            o_keep(n - 1, 3)
                        if p % 2 == 1 and p >= 3 and att:
                            o_keep(n, (p - 3) // 2)
                        if two and p == 4:
                            q_keep(1)
                    if one and p == 1:
                        act.wait_ge(xt_mm.sem, xt_mm.upto(n + 2))
                        act.wait_ge(qkv_mm.sem, qkv_mm.upto(n + 1))
                        copy(xt[:], bank["xt"][:, 0:SEQ]).then_inc(xt_sb.sem, 1)
                    if b:
                        if two and p == 2:
                            q_keep(0)
                            act.wait_ge(pv_mm.sem, pv_mm.upto(n - 1))
                            act.wait_ge(lo_sb.sem, lo_sb.upto(n + 1))
                            copy(v1[:, (k + 1) % 2, :, 0:8, 0:VW],
                                           qkv[:, 2, :, :].rearrange("p c (h d) -> p c h d", d=VW)).then_inc(v_sb.sem, 1)
                        if one and p in (3, 4):
                            c = p - 3
                            act.wait_ge(qkv_mm.sem, qkv_mm.upto(n + 2, c + 1))
                            act.wait_ge(v_sb.sem, v_sb.upto(n + 1))
                            act.wait_ge(rot.sem, rot.upto(n + 1))
                            copy(qkv[:, :, c, :], bank["qkv"][:, 0:3 * P].rearrange(
                                "p (a d) -> p a d", a=3)).then_inc(qkv_sb.sem, 1)
                    if a and one and p == 5:
                        act.wait_ge(qkv_sb.sem, qkv_sb.upto(n + 2))
                        act.wait_ge(ss_sb.sem, ss_sb.upto(n + 1))
                        act.activation(sq[:], qkv[:, 0:2, :, :].rearrange("p a c d -> p (a c d)"),
                                                  ACT.Square).then_inc(sq_sb.sem, 1)
                    if out and p == 6:
                        act.wait_ge(atr_mm.sem, atr_mm.upto(n - 1))
                        copy(at[:], bank["atr"][:, 0:SEQ]).then_inc(at_sb.sem, 1)
                    if b and two and p == 7:
                        q_final_keep(0)
                        q_final_keep(1)

            march(act, body)

        @block.gpsimd
        def _(pool):
            def body(n, k):
                one, two, att, out = doing(k)
                if a and one:
                    pool.wait_ge(xn_sb.sem, xn_sb.upto(n + 2))
                    pool.tensor_tensor(X2[:, (n + 2).at, :].rearrange("p (c d) -> p c d", c=2),
                                                  X2[:, (n + 2).at, :].rearrange("p (c d) -> p c d", c=2),
                                                  bc(g.bproj[:].unsqueeze(1), [P, 2, DIM]), ALU.add).then_inc(xb_sb.sem, 1)
                if b and out:
                    pool.wait_ge(a2_sb.sem, a2_sb.upto(n - 1))
                    pool.tensor_tensor(g.s_sq2[:], a2[:, :, :].rearrange("p c d -> p (c d)"),
                                                   a2[:, :, :].rearrange("p c d -> p (c d)"), ALU.mult).then_inc(sq2_sb.sem, 1)
                    pool.wait_ge(var_sb.sem, var_sb.upto(n - 1))
                    pool.tensor_tensor(g.s_inv2[:], g.s_var2[:], g.minus_half[:, 0:16], ALU.pow).then_inc(inv2_sb.sem, 1)
                if a and one:
                    pool.wait_ge(seed.sem, seed.upto(n + 2))
                    i = 0
                    for it in range(3):
                        for o, u, w, op in ((yt, y, y, ALU.mult), (yt, yt, vh, ALU.mult),
                                            (yt, yt, g.three_halves, ALU.add), (y, y, yt, ALU.mult)):
                            if i:
                                pool.wait_ge(newton.sem, newton.upto(n + 2, i))
                            pool.tensor_tensor(o[:], u[:], w[:], op).then_inc(newton.sem, 1)
                            i += 1
                if b and one:
                    pool.wait_ge(qkv_sb.sem, qkv_sb.upto(n + 2))
                    pool.wait_ge(qh_sb.sem, qh_sb.upto(n + 1))
                    flat = qkv[:, 0:2, :, :].rearrange("p a c d -> p (a c d)")
                    pool.tensor_tensor(g.s_rot[:, 0, :], flat, g.rope_cos[:], ALU.mult).then_inc(rot.sem, 1)
                    pool.tensor_tensor(
                        g.s_rot[:, 1, :].rearrange("p (i e) -> p i e", e=2),
                        flat.rearrange("p (i e) -> p i e", e=2)[:, :, ::-1],
                        g.rope_sin[:].rearrange("p (i e) -> p i e", e=2), ALU.mult).then_inc(rot.sem, 1)
                if one:
                    for i, dst in enumerate((qs, ks)):
                        pool.wait_ge(hi_sb.sem, hi_sb.upto(n + 2, i + 1))
                        d4 = dst[:, k % 2, :, :].rearrange("p c (h s d) -> p (c h) s d", s=4, d=HD)
                        pool.tensor_tensor(d4[:, :, 2 if i == 0 else 1, :],
                                                      qh[:, i, :].rearrange("p (h d) -> p h d", d=HD),
                                                      d4[:, :, 0, :], ALU.subtract).then_inc(lo_sb.sem, 1)
                if out:
                    pool.wait_ge(vare_sb.sem, vare_sb.upto(n - 1))
                    pool.tensor_tensor(rstd_next[:, :].rearrange("p (n c) -> p n c", c=2)[:, (n - 1).at, :],
                                                    g.s_vare[:], g.minus_half[:, 0:2], ALU.pow).then_inc(rstd_sb.sem, 1)

            march(pool, body)

        @block.vector
        def _(dve):
            dve.memset(qs[:], 0.0)
            dve.memset(ks[:], 0.0)
            dve.memset(v1[:], 0.0).then_inc(filled.sem, 1)
            dve.wait_ge(filled.sem, filled.upto(Step(None, 0, 0)))
            dve.memset(v1[:, :, :, :, VW:VW + 1], 1.0).then_inc(filled.sem, 1)
            if b:
                dve.memset(ks[:].rearrange("p r c (h s) -> p (r c h) s", s=32)[:, :, 24:25], 1.0).then_inc(filled.sem, 1)
                dve.wait_ge(filled.sem, filled.upto(Step(None, 0, 2)))
            else:
                dve.wait_ge(filled.sem, filled.upto(Step(None, 0, 1)))

            def body(n, k):
                one, two, att, out = doing(k)
                before = 0 <= k - 1 < NSEQ

                def normalise():
                    dve.wait_ge(xt_mm.sem, xt_mm.upto(n + 1))
                    for c in range(2):
                        t = ((n + 2) * 2 + c).at
                        dve.tensor_scalar(xn[:, c, :], g.x[:, t, :], mean[:, t:t + 1] if isinstance(t, int) else mean[:, :].rearrange("p (n c) -> p n c", c=2)[:, (n + 2).at, c:c + 1],
                                                     rstd2(rstd, n + 2, c), ALU.subtract, ALU.mult).then_inc(xn_sb.sem, 1)

                def split(i, dst):
                    d4 = dst[:, k % 2, :, :].rearrange("p c (h s d) -> p (c h) s d", s=4, d=HD)
                    o = d4[:, :, 0:2, :] if i == 0 else d4[:, :, 0:3:2, :]
                    src = qh[:, i, :].rearrange("p (h d) -> p h d", d=HD).unsqueeze(2)
                    dve.tensor_copy(o.bitcast(F32R), bc(src, [P, 32, 2, HD])).then_inc(hi_sb.sem, 1)

                def operands():
                    q_seen = qp_mm if a else qf_mm
                    dve.wait_ge(q_seen.sem, q_seen.upto(n))
                    dve.wait_ge(kt_mm.sem, kt_mm.upto(n))
                    if a:
                        dve.wait_ge(newton.sem, newton.upto(n + 2))
                        dve.wait_ge(lo_sb.sem, lo_sb.upto(n + 1))
                        flat = qkv[:, 0:2, :, :].rearrange("p a c (h d) -> p (a c h) d", d=HD)
                        dve.tensor_tensor(qh[:].rearrange("p a (h d) -> p (a h) d", d=HD), flat,
                                                     bc(y[:].unsqueeze(2), [P, 64, HD]), ALU.mult).then_inc(qh_sb.sem, 1)
                        dve.wait_ge(qh_sb.sem, qh_sb.upto(n + 2, 1))
                        qc = qh[:, 0, :].rearrange("p (c d) -> p c d", c=2)
                        dve.tensor_tensor(qc, qc, bc(g.qk_scale[:].unsqueeze(1), [P, 2, DIM]), ALU.mult).then_inc(qh_sb.sem, 1)
                    else:
                        dve.wait_ge(rot.sem, rot.upto(n + 2))
                        dve.wait_ge(lo_sb.sem, lo_sb.upto(n + 1))
                        dve.tensor_tensor(qh[:].rearrange("p a d -> p (a d)"), g.s_rot[:, 0, :],
                                                     g.s_rot[:, 1, :], ALU.add).then_inc(qh_sb.sem, 1)
                    dve.wait_ge(qh_sb.sem, qh_sb.upto(n + 2))
                    split(0, qs)
                    split(1, ks)

                def tokens(c):
                    dve.wait_ge(otr_mm.sem, otr_mm.upto(n - 1, c + 1))
                    o3 = bank["otr"].rearrange("p (h s) -> p h s", s=32)
                    dve.reciprocal(rs[:].unsqueeze(2), o3[:, :, VW:VW + 1]).then_inc(rs_sb.sem, 1)
                    dve.wait_ge(rs_sb.sem, rs_sb.upto(n - 1, 2 * c + 1))
                    if a:
                        dve.tensor_copy(g.s_pad[:, 0:1], rs[:, 0:1]).then_inc(rs_sb.sem, 1)
                        dve.wait_ge(atr_mm.sem, atr_mm.upto(n - 2))
                        dve.tensor_tensor(an[:, c, :].rearrange("p (h d) -> p h d", d=HD),
                                                        o3[:, :, 0:VW], bc(rs[:].unsqueeze(2), [P, HEADS, VW]),
                                                        ALU.mult).then_inc(otr_used.sem, 1)
                        return
                    odd = rs[:].rearrange("p (h e) -> p h e", e=2)[:, :, 1:2]
                    dve.tensor_scalar(odd, odd, g.minus_lam[:], None, ALU.mult).then_inc(rs_sb.sem, 1)
                    dve.wait_ge(rs_sb.sem, rs_sb.upto(n - 1, 2 * c + 2))
                    dve.tensor_tensor(tv[:].rearrange("p (h d) -> p h d", d=VW), o3[:, :, 0:VW],
                                                    bc(rs[:].unsqueeze(2), [P, HEADS, VW]), ALU.mult).then_inc(otr_used.sem, 1)
                    dve.wait_ge(otr_used.sem, otr_used.upto(n - 1, c + 1))
                    t4 = tv[:].rearrange("p (h e d) -> p h e d", e=2, d=VW)
                    dve.wait_ge(inv2_sb.sem, inv2_sb.upto(n - 2))
                    dve.tensor_tensor(a2[:, c, :].rearrange("p (h d) -> p h d", d=VW),
                                                 t4[:, :, 0, :], t4[:, :, 1, :], ALU.add).then_inc(a2_sb.sem, 1)

                def mean_square():
                    dve.wait_ge(sq2_sb.sem, sq2_sb.upto(n - 1))
                    dve.tensor_reduce(g.s_ms2[:], g.s_sq2[:].rearrange("p (h d) -> p h d", d=16),
                                                 AX.X, ALU.add).then_inc(ms_sb.sem, 1)
                    dve.wait_ge(ms_sb.sem, ms_sb.upto(n - 1))
                    dve.tensor_scalar(g.s_var2[:], g.s_ms2[:], 1.0 / 16, RMS_EPS_B, ALU.mult, ALU.add).then_inc(var_sb.sem, 1)

                def head_norm():
                    dve.wait_ge(inv2_sb.sem, inv2_sb.upto(n - 1))
                    dve.wait_ge(atr_mm.sem, atr_mm.upto(n - 2))
                    for c in range(2):
                        dve.scalar_tensor_tensor(
                            out=an[:, c, :].rearrange("p (h d) -> p h d", d=16),
                            in0=a2[:, c, :].rearrange("p (h d) -> p h d", d=16), scalar=1.0 - LAMBDA_INIT,
                            in1=bc(g.s_inv2[:, 8 * c:8 * c + 8].unsqueeze(2), [P, 8, 16]),
                            op0=ALU.mult, op1=ALU.mult).then_inc(an_sb.sem, 1)

                def residual():
                    dve.wait_ge(pj_mm.sem, pj_mm.upto(n - 1))
                    if a:
                        dve.wait_ge(xb_sb.sem, xb_sb.upto(n - 1))
                    dve.tensor_tensor(X2[:, (n - 1).at, :], bank["pj"][:, 0:SEQ], X2[:, (n - 1).at, :], ALU.add).then_inc(x_sb.sem, 1)
                    dve.wait_ge(x_sb.sem, x_sb.upto(n - 1))
                    dve.wait_ge(rstd_sb.sem, rstd_sb.upto(n - 2))
                    dve.memset(g.s_pad[:, 3:4], 0.0)
                    for c in range(2):
                        ins = dve.bn_stats(g.s_bn[:, c, :], g.x[:, (n * 2 - 2 + c).at, :])
                    ins.then_inc(bn_sb.sem, 1)
                    dve.wait_ge(bn_sb.sem, bn_sb.upto(n - 1))
                    dve.memset(g.s_pad[:, 3:4], 0.0)
                    for c in range(2):
                        ins = dve.bn_aggr(g.s_mv[:, c, :], g.s_bn[:, c, :])
                    ins.then_inc(mv_sb.sem, 1)
                    dve.wait_ge(mv_sb.sem, mv_sb.upto(n - 1))
                    dve.tensor_scalar(g.s_vare[:], g.s_mv[:, 0:2, 1], LN_EPS, None, ALU.add).then_inc(vare_sb.sem, 1)
                    dve.tensor_copy(mean_next[:, :].rearrange("p (n c) -> p n c", c=2)[:, (n - 1).at, :],
                                    g.s_mv[:, 0:2, 0])

                def o_keep(m, q):
                    dve.wait_ge(pv_mm.sem, pv_mm.upto(m, 2 * q + 2))
                    if q == 0:
                        dve.wait_ge(otr_mm.sem, otr_mm.upto(m - 1))
                    dve.tensor_copy(ot[:, q, :], PV).then_inc(ot_sb.sem, 1)

                for p in range(PAIRS):
                    if one and p == 0:
                        normalise()
                    if a:
                        if out and p in (2, 3):
                            tokens(p - 2)
                            if p == 3:
                                dve.wait_ge(otr_used.sem, otr_used.upto(n - 1))
                                dve.tensor_copy(g.s_pad[:, 1:2], an[:, 0, 0:1]).then_inc(an_sb.sem, 1)
                                dve.tensor_copy(g.s_pad[:, 2:3], an[:, 1, 0:1]).then_inc(an_sb.sem, 1)
                        if p == 1 and before:
                            o_keep(n - 1, 3)
                        if p % 2 == 1 and p >= 3 and att:
                            o_keep(n, (p - 3) // 2)
                        if two and p == 2:
                            dve.wait_ge(pv_mm.sem, pv_mm.upto(n - 1))
                            dve.tensor_copy(v1[:, (k + 1) % 2, :, :, 0:VW],
                                                      qkv[:, 2, :, :].rearrange("p c (h d) -> p c h d", d=VW)).then_inc(v_sb.sem, 1)
                        if one and p in (2, 3):
                            c = p - 2
                            dve.wait_ge(qkv_mm.sem, qkv_mm.upto(n + 2, c + 1))
                            dve.wait_ge(v_sb.sem, v_sb.upto(n + 1))
                            dve.tensor_tensor(
                                qkv[:, :, c, :], bank["qkv"][:, 0:3 * P].rearrange("p (a d) -> p a d", a=3),
                                g.bqkv[:].rearrange("p (a d) -> p a d", a=3), ALU.add).then_inc(qkv_sb.sem, 1)
                        if two and p in (4, 5):
                            c = p - 4
                            dve.wait_ge(qp_mm.sem, qp_mm.upto(n + 1, c + 1))
                            dve.tensor_copy(qt[:, (k + 1) % 2, :, c * P:(c + 1) * P],
                                                       bank["qp"].rearrange("p (q t) -> p q t", q=4)).then_inc(qp_sb.sem, 1)
                        if one and p == 5:
                            dve.wait_ge(sq_sb.sem, sq_sb.upto(n + 2))
                            dve.wait_ge(newton.sem, newton.upto(n + 1))
                            dve.tensor_reduce(ss[:], sq[:].rearrange("p (h d) -> p h d", d=HD),
                                                         AX.X, ALU.add).then_inc(ss_sb.sem, 1)
                            dve.wait_ge(ss_sb.sem, ss_sb.upto(n + 2))
                            dve.tensor_scalar(g.s_v[:], ss[:], 1.0 / HD, RMS_EPS_A, ALU.mult, ALU.add).then_inc(seed.sem, 1)
                            dve.wait_ge(seed.sem, seed.upto(n + 2, 1))
                            dve.tensor_scalar(vh[:], g.s_v[:], -0.5, None, ALU.mult).then_inc(seed.sem, 1)
                            dve.tensor_scalar(g.s_i[:], g.s_v[:].bitcast(I32), 1, None,
                                                        ALU.logical_shift_right).then_inc(seed.sem, 1)
                            dve.wait_ge(seed.sem, seed.upto(n + 2, 3))
                            dve.tensor_scalar(y[:].bitcast(I32), g.s_i[:], -1.0, float(0x5F3759DF),
                                                        ALU.mult, ALU.add).then_inc(seed.sem, 1)
                        if out and p == 7:
                            residual()
                        if one and p == 7:
                            operands()
                    else:
                        if out and p in (2, 3):
                            tokens(p - 2)
                        if out and p == 5:
                            mean_square()
                        if out and p == 6:
                            head_norm()
                        if one and p == 6:
                            operands()
                        if out and p == 7:
                            residual()
                        if two:
                            for u in range(UNITS):
                                if sum(UNITS_AT.get(z, 0) for z in range(p)) <= u < sum(
                                        UNITS_AT.get(z, 0) for z in range(p + 1)):
                                    c, v = u // 8, u % 8
                                    r, pair = v % 4, v // 4
                                    o = qs[:, (k + 1) % 2, c, :].rearrange("p (q r s) -> p q r s", q=4, r=4)
                                    dve.wait_ge(mx_mm.sem, mx_mm.upto(n + 1, u + 1))
                                    dve.wait_ge(lo_sb.sem, lo_sb.upto(n + 1))
                                    dve.tensor_reduce(
                                        o[:, 2 * pair:2 * pair + 2, r, 24:25].bitcast(F32R),
                                        M[u % 2].rearrange("p (j s) -> p j s", j=2), AX.X, ALU.max, negate=True).then_inc(mx_sb.sem, 1)

            march(dve, body)


def rstd2(rstd, n, c):
    return rstd[:, :].rearrange("p (n c) -> p n c", c=2)[:, n.at, c:c + 1]


def feed_forward(nc, ctx, g, tag, psum, out):
    first = tag == "f"
    mean, rstd = (g.mean[1], g.rstd[1]) if first else (g.mean[3], g.rstd[3])
    mean_next, rstd_next = g.mean[2], g.rstd[2]
    X4 = g.x[:, :, :].rearrange("p (n c) d -> p n (c d)", c=4)
    xn, xt, st, ssp = g.f_xn, g.f_xt, g.f_st, g.f_ss
    T, SB = psum[:, 0:512], psum[:, 512:1024]
    H1 = [psum[:, 1024:1536], psum[:, 1536:2048]]
    H3 = [psum[:, 2048:2560], psum[:, 2560:3072]]
    Y = [psum[:, 3072:3584], psum[:, 3584:4096]]
    NE = E + 1

    def ev(name, per):
        return Events(ctx, nc, f"{tag}_{name}", per)

    filled = ev("filled", 1)
    xn_sb, xt_mm, xt_sb, lg_mm, lg_sb = ev("xn_sb", 4), ev("xt_mm", 1), ev("xt_sb", 1), ev("lg_mm", 1), ev("lg_sb", 1)
    top_sb, idx_sb, ix_sb, sh_sb, pw_sb = ev("top_sb", 1), ev("idx_sb", 1), ev("ix_sb", 1), ev("sh_sb", 1), ev("pw_sb", 1)
    gs_sb, m_sb, sc_sb, hi_sb, lo_sb = ev("gs_sb", 2), ev("m_sb", 3), ev("sc_sb", 2), ev("hi_sb", 1), ev("lo_sb", 1)
    st_mm, st_sb = ev("st_mm", 1), ev("st_sb", 1)
    sb_mm, xe_sb = ev("sb_mm", E), ev("xe_sb", E)
    h1_mm, h3_mm, g_sb, h_sb = ev("h1_mm", NE), ev("h3_mm", NE), ev("g_sb", NE), ev("h_sb", NE)
    y_mm, x_sb = ev("y_mm", NE), ev("x_sb", 1)
    bn_sb, mv_sb, vare_sb, rstd_sb = ev("bn_sb", 1), ev("mv_sb", 1), ev("vare_sb", 1), ev("rstd_sb", 1)
    stored = ctx.enter_context(nc.semaphore(f"{tag}_stored"))

    def march(eng, body):
        for n in (-1, 0):
            body(Step(None, 0, n), n)
        with eng.Fori(0, 3) as i:
            body(Step(i, 2, 1), 1)
            body(Step(i, 2, 2), 2)
        body(Step(None, 0, 7), 7)

    def doing(k):
        return k + 1 < NCH, 0 <= k

    with nc.Block() as block:

        @block.tensor
        def _(pe):
            def body(n, k):
                gate, run = doing(k)
                par = k % 2

                def spread(e):
                    if e == 0:
                        pe.wait_ge(st_sb.sem, st_sb.upto(n))
                    if e == 0:
                        pe.wait_ge(xe_sb.sem, xe_sb.upto(n - 1))
                    else:
                        pe.wait_ge(xe_sb.sem, xe_sb.upto(n, e))
                    pe.matmul(SB, g.select[:, e, :], st[:, par, :], start=True, stop=True).then_inc(sb_mm.sem, 1)

                def up(e):
                    if e < E:
                        pe.wait_ge(xe_sb.sem, xe_sb.upto(n, e + 1))
                        src = g.f_xe[:, e % 2, :]
                    else:
                        src = xt[:, par, :]
                    q = (e + k) % 2
                    if e >= 2:
                        pe.wait_ge(g_sb.sem, g_sb.upto(n, e - 1))
                    elif k > 0:
                        pe.wait_ge(g_sb.sem, g_sb.upto(n - 1, 8 + e))
                    pe.matmul(H1[q], g.w1[:, e, :], src, start=True, stop=True).then_inc(h1_mm.sem, 1)
                    if e >= 2:
                        pe.wait_ge(h_sb.sem, h_sb.upto(n, e - 1))
                    elif k > 0:
                        pe.wait_ge(h_sb.sem, h_sb.upto(n - 1, 8 + e))
                    pe.matmul(H3[q], g.w3[:, e, :], src, start=True, stop=True).then_inc(h3_mm.sem, 1)

                def down(e):
                    pe.wait_ge(h_sb.sem, h_sb.upto(n, e + 1))
                    if e == 0:
                        pe.wait_ge(x_sb.sem, x_sb.upto(n - 1))
                    q = (e + k) % 2
                    for t in range(4):
                        ins = pe.matmul(Y[par][:, t * P:(t + 1) * P], g.f_h[:, q, t * P:(t + 1) * P], g.w2[:, e, :],
                                        start=(e == 0 and t == 0), stop=(e == NE - 1 and t == 3),
                                        skip_group_check=True)
                    ins.then_inc(y_mm.sem, 1)

                def x_turn():
                    pe.wait_ge(xn_sb.sem, xn_sb.upto(n + 1))
                    pe.wait_ge(st_sb.sem, st_sb.upto(n))
                    for t in range(4):
                        ins = pe.transpose(T[:, t * P:(t + 1) * P], xn[:, t, :], g.identity[:])
                    ins.then_inc(xt_mm.sem, 1)

                def logits():
                    pe.wait_ge(xt_sb.sem, xt_sb.upto(n + 1))
                    for t in range(4):
                        ins = pe.matmul(T[:, t * E:(t + 1) * E], xt[:, (k + 1) % 2, t * P:(t + 1) * P], g.gate[:],
                                        start=True, stop=True)
                    ins.then_inc(lg_mm.sem, 1)

                def s_turn():
                    pe.wait_ge(lo_sb.sem, lo_sb.upto(n + 1))
                    for t in range(4):
                        ins = pe.transpose(T[:, t * P:(t + 1) * P], ssp[:, t, :], g.identity[:])
                    ins.then_inc(st_mm.sem, 1)

                if run:
                    spread(0)
                    up(0)
                for e in range(NE):
                    if run:
                        if e + 1 < E:
                            spread(e + 1)
                        if e + 1 < NE:
                            up(e + 1)
                    if gate and e == 0:
                        x_turn()
                    if gate and e == 1:
                        logits()
                    if gate and e == 6:
                        s_turn()
                    if run:
                        down(e)

            march(pe, body)

        @block.scalar
        def _(act):
            def body(n, k):
                gate, run = doing(k)
                for e in range(NE):
                    if run:
                        act.wait_ge(h1_mm.sem, h1_mm.upto(n, e + 1))
                        if e >= 2:
                            act.wait_ge(h_sb.sem, h_sb.upto(n, e - 1))
                        elif k > 0:
                            act.wait_ge(h_sb.sem, h_sb.upto(n - 1, 8 + e))
                        q = (e + k) % 2
                        act.activation(g.f_g[:, q, :], H1[q], ACT.Silu).then_inc(g_sb.sem, 1)
                    if gate and e == 0:
                        act.wait_ge(xt_mm.sem, xt_mm.upto(n + 1))
                        if k > 0:
                            act.wait_ge(h3_mm.sem, h3_mm.upto(n - 1))
                        act.activation(xt[:, (k + 1) % 2, :], T, ACT.Copy).then_inc(xt_sb.sem, 1)
                    if gate and e == 6:
                        act.wait_ge(st_mm.sem, st_mm.upto(n + 1))
                        act.activation(st[:, (k + 1) % 2, :], T, ACT.Copy).then_inc(st_sb.sem, 1)

            march(act, body)

        @block.gpsimd
        def _(pool):
            def body(n, k):
                gate, run = doing(k)
                if gate:
                    pool.wait_ge(sh_sb.sem, sh_sb.upto(n + 1))
                    pool.tensor_tensor(g.f_p[:], g.euler[:], g.f_sh[:], ALU.pow).then_inc(pw_sb.sem, 1)
                if run and first:
                    pool.wait_ge(vare_sb.sem, vare_sb.upto(n))
                    pool.tensor_tensor(
                        rstd_next[:, :].rearrange("p (n c) -> p n c", c=4)[:, n.at, :], g.f_vare[:],
                        g.minus_half[:, 0:4], ALU.pow).then_inc(rstd_sb.sem, 1)

            march(pool, body)

        @block.vector
        def _(dve):
            dve.memset(ssp[:], 0.0).then_inc(filled.sem, 1)
            dve.wait_ge(filled.sem, filled.upto(Step(None, 0, 0)))

            def body(n, k):
                gate, run = doing(k)
                par = k % 2

                def scale(e):
                    dve.wait_ge(sb_mm.sem, sb_mm.upto(n, e + 1))
                    if e >= 2:
                        dve.wait_ge(h3_mm.sem, h3_mm.upto(n, e - 1))
                    dve.tensor_tensor(g.f_xe[:, e % 2, :], SB, xt[:, par, :], ALU.mult).then_inc(xe_sb.sem, 1)

                def hidden(e):
                    dve.wait_ge(g_sb.sem, g_sb.upto(n, e + 1))
                    dve.wait_ge(h3_mm.sem, h3_mm.upto(n, e + 1))
                    if e >= 2:
                        dve.wait_ge(y_mm.sem, y_mm.upto(n, e - 1))
                    elif k > 0:
                        dve.wait_ge(y_mm.sem, y_mm.upto(n - 1, 8 + e))
                    q = (e + k) % 2
                    dve.tensor_tensor(g.f_h[:, q, :], H3[q], g.f_g[:, q, :], ALU.mult).then_inc(h_sb.sem, 1)

                def normalise():
                    dve.wait_ge(xt_mm.sem, xt_mm.upto(n))
                    for c in range(4):
                        dve.tensor_scalar(
                            xn[:, c, :], g.x[:, ((n + 1) * 4 + c).at, :],
                            mean[:, :].rearrange("p (n c) -> p n c", c=4)[:, (n + 1).at, c:c + 1],
                            rstd[:, :].rearrange("p (n c) -> p n c", c=4)[:, (n + 1).at, c:c + 1],
                            ALU.subtract, ALU.mult).then_inc(xn_sb.sem, 1)

                def best():
                    dve.wait_ge(lg_mm.sem, lg_mm.upto(n + 1))
                    dve.tensor_copy(g.f_lg[:], T[:, 0:4 * E]).then_inc(lg_sb.sem, 1)
                    dve.wait_ge(lg_sb.sem, lg_sb.upto(n + 1))
                    dve.memset(g.s_pad[:, 0:1], 0.0)
                    for t in range(4):
                        ins = dve.max(g.f_top[:, t, :], g.f_lg[:, t * E:(t + 1) * E])
                    ins.then_inc(top_sb.sem, 1)
                    dve.wait_ge(top_sb.sem, top_sb.upto(n + 1))
                    dve.memset(g.s_pad[:, 1:2], 0.0)
                    for t in range(4):
                        ins = dve.max_index(g.f_idx[:, t, :], g.f_top[:, t, :], g.f_lg[:, t * E:(t + 1) * E])
                    ins.then_inc(idx_sb.sem, 1)
                    l3 = g.f_lg[:].rearrange("p (t e) -> p t e", e=E)
                    dve.tensor_tensor(g.f_sh[:].rearrange("p (t e) -> p t e", e=E), l3,
                                                 bc(g.f_top[:, :, 0:1], [P, 4, E]), ALU.subtract).then_inc(sh_sb.sem, 1)
                    dve.wait_ge(idx_sb.sem, idx_sb.upto(n + 1))
                    dve.tensor_copy(g.f_ix[:], g.f_idx[:, :, 0:2]).then_inc(ix_sb.sem, 1)
                    dve.wait_ge(ix_sb.sem, ix_sb.upto(n + 1))
                    for j in range(2):
                        dve.tensor_tensor(g.f_m[:, j, :, :], bc(g.iota[:].unsqueeze(1), [P, 4, E]),
                                                    bc(g.f_ix[:, :, j:j + 1], [P, 4, E]), ALU.is_equal).then_inc(m_sb.sem, 1)
                    dve.wait_ge(m_sb.sem, m_sb.upto(n + 1, 2))
                    dve.tensor_tensor(g.f_m[:, 0, :, :], g.f_m[:, 0, :, :], g.f_m[:, 1, :, :], ALU.add).then_inc(m_sb.sem, 1)

                def gates():
                    dve.wait_ge(pw_sb.sem, pw_sb.upto(n + 1))
                    p3 = g.f_p[:].rearrange("p (t e) -> p t e", e=E)
                    dve.tensor_reduce(g.f_sum[:], p3, AX.X, ALU.add).then_inc(gs_sb.sem, 1)
                    dve.wait_ge(gs_sb.sem, gs_sb.upto(n + 1, 1))
                    dve.reciprocal(g.f_rs[:], g.f_sum[:]).then_inc(gs_sb.sem, 1)
                    dve.wait_ge(m_sb.sem, m_sb.upto(n + 1))
                    dve.tensor_tensor(g.f_m[:, 1, :, :], p3, g.f_m[:, 0, :, :], ALU.mult).then_inc(sc_sb.sem, 1)
                    dve.wait_ge(gs_sb.sem, gs_sb.upto(n + 1))
                    dve.wait_ge(sc_sb.sem, sc_sb.upto(n + 1, 1))
                    dve.tensor_tensor(g.f_m[:, 0, :, :], g.f_m[:, 1, :, :],
                                                 bc(g.f_rs[:].unsqueeze(2), [P, 4, E]), ALU.mult).then_inc(sc_sb.sem, 1)
                    dve.wait_ge(sc_sb.sem, sc_sb.upto(n + 1))
                    dve.wait_ge(st_mm.sem, st_mm.upto(n))
                    dve.tensor_copy(ssp[:, :, 0:E].bitcast(F32R), g.f_m[:, 0, :, :]).then_inc(hi_sb.sem, 1)
                    dve.wait_ge(hi_sb.sem, hi_sb.upto(n + 1))
                    dve.tensor_tensor(ssp[:, :, E:2 * E], g.f_m[:, 0, :, :], ssp[:, :, 0:E], ALU.subtract).then_inc(lo_sb.sem, 1)

                def residual():
                    dve.wait_ge(y_mm.sem, y_mm.upto(n))
                    dve.tensor_tensor(X4[:, n.at, :], Y[par], X4[:, n.at, :], ALU.add).then_inc(x_sb.sem, 1)
                    if first:
                        dve.wait_ge(x_sb.sem, x_sb.upto(n))
                        dve.wait_ge(rstd_sb.sem, rstd_sb.upto(n - 1))
                        dve.memset(g.s_pad[:, 3:4], 0.0)
                        for c in range(4):
                            ins = dve.bn_stats(g.f_bn[:, c, :], g.x[:, (n * 4 + c).at, :])
                        ins.then_inc(bn_sb.sem, 1)
                        dve.wait_ge(bn_sb.sem, bn_sb.upto(n))
                        dve.memset(g.s_pad[:, 3:4], 0.0)
                        for c in range(4):
                            ins = dve.bn_aggr(g.s_mv[:, c, :], g.f_bn[:, c, :])
                        ins.then_inc(mv_sb.sem, 1)
                        dve.wait_ge(mv_sb.sem, mv_sb.upto(n))
                        dve.tensor_scalar(g.f_vare[:], g.s_mv[:, :, 1], LN_EPS, None, ALU.add).then_inc(vare_sb.sem, 1)
                        dve.tensor_copy(mean_next[:, :].rearrange("p (n c) -> p n c", c=4)[:, n.at, :],
                                        g.s_mv[:, :, 0])

                if run:
                    scale(0)
                if gate:
                    normalise()
                for e in range(NE):
                    if run and e + 1 < E:
                        scale(e + 1)
                    if gate and e == 2:
                        best()
                    if gate and e == 5:
                        gates()
                    if run:
                        hidden(e)
                if run:
                    residual()

            march(dve, body)

        if not first:
            @block.sync
            def _(sp):
                view = out.rearrange("(n s) (c p) d -> n p (s c) d", s=2, p=P)
                with sp.Fori(0, NCH) as n:
                    sp.wait_ge(x_sb.sem, x_sb.upto(Step(n, 1, 0)))
                    sp.dma_start(view[n], g.x[:, :, :].rearrange("p (n c) d -> p n c d", c=4)[:, n, :, :]
                                 ).then_inc(stored, 16)
                sp.wait_ge(stored, 16 * NCH)


def program(nc, d, out):
    with ExitStack() as ctx:
        g = Shared()

        def sb(name, shape, dt=F32):
            return ctx.enter_context(nc.sbuf_tensor(name, shape, dt))

        g.x = sb("x", [P, NT, DIM])
        g.mean = [sb(f"mean{i}", [P, NT]) for i in range(4)]
        g.s_mv = sb("s_mv", [P, 4, 2])
        g.rstd = [sb(f"rstd{i}", [P, NT]) for i in range(4)]
        g.identity = sb("identity", [P, P])
        g.wqkv_a, g.wqkv_b = sb("wqkv_a", [P, 3 * P]), sb("wqkv_b", [P, 3 * P])
        g.bqkv, g.bproj = sb("bqkv", [P, 3 * P]), sb("bproj", [P, DIM])
        g.qk_w, g.qk_scale = sb("qk_w", [P, 2, HD]), sb("qk_scale", [P, DIM])
        g.minus_bound, g.minus_lam = sb("minus_bound", [P, 1]), sb("minus_lam", [P, 1])
        g.wproj, g.wo = sb("wproj", [P, DIM]), sb("wo", [P, DIM])
        g.lam_in = sb("lam_in", [P, 4, HD])
        g.select_raw, g.select = sb("select_raw", [P, E, P]), sb("select", [P, E, P], F32R)
        g.iota, g.gate = sb("iota", [P, E]), sb("gate", [P, E])
        g.w1, g.w3, g.w2 = (sb(x, [P, E + 1, P]) for x in ("w1", "w3", "w2"))
        g.rope_cos, g.rope_sin = sb("rope_cos", [P, 512]), sb("rope_sin", [P, 512])
        g.minus_half, g.three_halves = sb("minus_half", [P, 16]), sb("three_halves", [P, 64])
        g.euler, g.ln_eps = sb("euler", [P, 32]), sb("ln_eps", [P, 4])
        g.s_xn, g.s_xt = sb("s_xn", [P, 2, DIM]), sb("s_xt", [P, SEQ])
        g.s_qkv, g.s_qh = sb("s_qkv", [P, 3, 2, P]), sb("s_qh", [P, 2, 256])
        g.s_qs, g.s_ks = sb("s_qs", [P, 2, 2, 512]), sb("s_ks", [P, 2, 2, 512])
        g.s_v1 = sb("s_v1", [P, 2, 2, HEADS, 32])
        g.s_kt, g.s_qt = sb("s_kt", [P, 2, 4, SEQ], F32R), sb("s_qt", [P, 2, 4, SEQ], F32R)
        g.s_qp = sb("s_qp", [P, 4, SEQ], F32R)
        g.s_probs = sb("s_probs", [P, 4, 2, 2, SEQ])
        g.s_ot, g.s_an, g.s_at = sb("s_ot", [P, 4, SEQ]), sb("s_an", [P, 2, DIM]), sb("s_at", [P, SEQ])
        g.s_sq, g.s_ss, g.s_vh = sb("s_sq", [P, 512]), sb("s_ss", [P, 64]), sb("s_vh", [P, 64])
        g.s_v, g.s_i, g.s_y, g.s_yt = sb("s_v", [P, 64]), sb("s_i", [P, 64], I32), sb("s_y", [P, 64]), sb("s_yt", [P, 64])
        g.s_rs, g.s_tv, g.s_a2 = sb("s_rs", [P, HEADS]), sb("s_tv", [P, 256]), sb("s_a2", [P, 2, DIM])
        g.s_rot, g.s_pad = sb("s_rot", [P, 2, 512]), sb("s_pad", [P, 4])
        g.s_sq2, g.s_ms2, g.s_var2, g.s_inv2 = (sb(x, [P, w]) for x, w in (
            ("s_sq2", 256), ("s_ms2", 16), ("s_var2", 16), ("s_inv2", 16)))
        g.s_bn, g.s_vare = sb("s_bn", [P, 2, 6]), sb("s_vare", [P, 2])
        g.f_xn, g.f_xt = sb("f_xn", [P, 4, DIM]), sb("f_xt", [P, 2, CH])
        g.f_ss, g.f_st = sb("f_ss", [P, 4, P]), sb("f_st", [P, 2, CH], F32R)
        g.f_xe, g.f_g, g.f_h = (sb(x, [P, 2, CH]) for x in ("f_xe", "f_g", "f_h"))
        g.f_lg, g.f_sh, g.f_p = (sb(x, [P, 4 * E]) for x in ("f_lg", "f_sh", "f_p"))
        g.f_top, g.f_idx, g.f_ix = sb("f_top", [P, 4, E]), sb("f_idx", [P, 4, E], U32), sb("f_ix", [P, 4, 2])
        g.f_m, g.f_sum, g.f_rs = sb("f_m", [P, 2, 4, E]), sb("f_sum", [P, 4]), sb("f_rs", [P, 4])
        g.f_bn, g.f_vare = sb("f_bn", [P, 4, 6]), sb("f_vare", [P, 4])
        psum = ctx.enter_context(nc.psum_tensor("psum", [P, 4096], F32))

        setup(nc, ctx, g, d)
        attention(nc, ctx, g, "a", psum)
        feed_forward(nc, ctx, g, "f", psum, None)
        attention(nc, ctx, g, "b", psum)
        feed_forward(nc, ctx, g, "h", psum, out)


def constants():
    identity = np.eye(P, dtype=np.float32)
    select = np.zeros((P, E, P), np.float32)
    for e in range(E):
        select[e, e, :] = 1.0
        select[E + e, e, :] = 1.0
    iota = np.tile(np.arange(E, dtype=np.float32), (P, 1))
    inv_freq = 1.0 / 10000.0 ** (np.arange(0, HD, 2, dtype=np.float64) / HD)
    pos = np.arange(SEQ, dtype=np.float64)
    freqs = np.repeat(np.float32(pos[:, None]) * np.float32(inv_freq[None, :]), 2, axis=-1).astype(np.float64)
    sv = (np.arange(0, HD, 2, dtype=np.float64) + 0.4 * HD) / (1.4 * HD)
    scale = sv[None, :] ** ((pos - SEQ // 2) / 512.0)[:, None]
    scale = np.concatenate([scale, scale], axis=-1)
    sign = np.where(np.arange(HD) % 2 == 0, -1.0, 1.0)

    def table(f):
        both = np.stack([f * scale * HD ** -0.5, f / scale])
        both = np.tile(both.reshape(2, 2, P, 1, HD), (1, 1, 1, HEADS, 1))
        return np.ascontiguousarray(both.transpose(2, 0, 1, 3, 4).reshape(P, 512).astype(np.float32))

    return {"identity": identity, "select": select, "iota": iota,
            "rope_cos": table(np.cos(freqs)), "rope_sin": table(np.sin(freqs) * sign)}


def kernel(**inputs):
    import concourse.bacc as bacc
    from concourse.bass_utils import run_bass_kernel_spmd

    def get(name):
        return np.asarray(inputs[name])

    arrays = {"x": get("L0_attn_a_x"),
              "Wqkv_aT": get("L0_attn_a_Wqkv").T, "WprojT": get("L0_attn_a_Wproj").T,
              "bqkv": get("L0_attn_a_bqkv"), "bproj": get("L0_attn_a_bproj"),
              "qn_w": get("L0_attn_a_qn_w"), "kn_w": get("L0_attn_a_kn_w"),
              "Wqkv_bT": np.concatenate([get(f"L0_attn_b_{w}").T for w in ("Wq", "Wk", "Wv")], axis=1),
              "WoT": get("L0_attn_b_Wo").T,
              "gate_wT": get("L0_ffn_gate_w").T}
    for w in ("lambda_q1", "lambda_k1", "lambda_q2", "lambda_k2"):
        arrays[w] = get(f"L0_attn_b_{w}")
    for w in ("w1", "w2", "w3", "w1s", "w2s", "w3s"):
        arrays[w] = get(f"L0_ffn_{w}")
    arrays.update(constants())

    nc = bacc.Bacc("TRN2", target_bir_lowering=False, num_devices=1)
    given, d = {}, {}
    for name, array in arrays.items():
        array = np.ascontiguousarray(array)
        given[f"in_{name}"] = array
        d[name] = nc.dram_tensor(f"in_{name}", array.shape, mybir.dt.from_np(array.dtype), kind="ExternalInput").ap()
    out = nc.dram_tensor("out_0", (NSEQ, SEQ, DIM), F32, kind="ExternalOutput").ap()
    program(nc, d, out)
    result = run_bass_kernel_spmd(nc, [given], core_ids=[0])
    return result.results[0]["out_0"]
```

```python
from contextlib import ExitStack

import numpy as np

import concourse.bass as bass
from concourse import mybir

F32 = mybir.dt.float32
F32R = mybir.dt.float32r
I32 = mybir.dt.int32
U32 = mybir.dt.uint32
ALU = mybir.AluOpType
ACT = mybir.ActivationFunctionType
AX = mybir.AxisListType

P = 128
NSEQ, SEQ, DIM = 16, 256, 128
NT = NSEQ * SEQ // P
HEADS = 16
HD = 8
LN_EPS = 1e-5
RMS_EPS_A = 1e-6
RMS_EPS_B = 1e-5
SCALE = 1.0 / float(np.sqrt(HD))
LAMBDA_INIT = 0.8 - 0.6 * float(np.exp(-0.3))
E = 8
NCH, CH = 8, 512
UNITS = 16


class Events:

    def __init__(self, ctx, nc, name, per):
        self.make = lambda: ctx.enter_context(nc.semaphore(name))
        self.taken = None
        self.per = per

    @property
    def sem(self):
        if self.taken is None:
            self.taken = self.make()
        return self.taken

    def upto(self, n, j=None):
        value = (n * self.per + (self.per if j is None else j)).at
        return max(value, 0) if isinstance(value, int) else value


class Step:

    def __init__(self, register, turns, offset):
        self.register, self.turns, self.offset = register, turns, offset

    def __add__(self, x):
        return Step(self.register, self.turns, self.offset + x)

    def __sub__(self, x):
        return self + -x

    def __mul__(self, x):
        return Step(self.register, self.turns * x, self.offset * x)

    @property
    def at(self):
        if self.register is None:
            return self.offset
        return self.register * self.turns + self.offset if self.offset else self.register * self.turns


class Shared:
    pass


def bc(ap, shape):
    return ap.broadcast_to(shape)


def setup(nc, ctx, g, d):
    x_view = d["x"].rearrange("b (c p) d -> p (b c) d", p=P)
    small_loads = [
        (g.qk_w[:, 0, :], d["qn_w"].partition_broadcast(P)),
        (g.qk_w[:, 1, :], d["kn_w"].partition_broadcast(P)),
        (g.lam_in[:, 0, :], d["lambda_q1"].partition_broadcast(P)),
        (g.lam_in[:, 1, :], d["lambda_q2"].partition_broadcast(P)),
        (g.lam_in[:, 2, :], d["lambda_k1"].partition_broadcast(P)),
        (g.lam_in[:, 3, :], d["lambda_k2"].partition_broadcast(P)),
        (g.identity[:], d["identity"]),
        (g.wqkv_a[:], d["Wqkv_aT"]),
        (g.bqkv[:], d["bqkv"].partition_broadcast(P)),
        (g.wproj[:], d["WprojT"]),
        (g.bproj[:], d["bproj"].partition_broadcast(P)),
    ]
    late_loads = [
        (g.w1[:, 0:E, :], d["w1"].rearrange("e p n -> p e n")),
        (g.w3[:, 0:E, :], d["w3"].rearrange("e p n -> p e n")),
        (g.w1[:, E, :], d["w1s"][0]),
        (g.w3[:, E, :], d["w3s"][0]),
        (g.select_raw[:], d["select"]),
        (g.w2[:, 0:E, :], d["w2"].rearrange("e p n -> p e n")),
        (g.w2[:, E, :], d["w2s"][0]),
        (g.iota[:], d["iota"]),
        (g.gate[:], d["gate_wT"]),
        (g.wqkv_b[:], d["Wqkv_bT"]),
        (g.wo[:], d["WoT"]),
        (g.rope_cos[:], d["rope_cos"]),
        (g.rope_sin[:], d["rope_sin"]),
    ]
    PARTS = 4
    W = NT // PARTS
    x_loaded = [ctx.enter_context(nc.semaphore(f"setup_x_loaded{i}")) for i in range(PARTS)]
    small_loaded = ctx.enter_context(nc.semaphore("setup_small_loaded"))
    g.late_loaded = ctx.enter_context(nc.semaphore("setup_late_loaded"))
    g.late_count = 16 * len(late_loads)
    zeroed = ctx.enter_context(nc.semaphore("setup_zeroed"))
    dve_step = ctx.enter_context(nc.semaphore("setup_dve_step"))
    var_ready = ctx.enter_context(nc.semaphore("setup_var_ready"))
    dev_ready = ctx.enter_context(nc.semaphore("setup_dev_ready"))
    dots_ready = ctx.enter_context(nc.semaphore("setup_dots_ready"))
    lam_ready = ctx.enter_context(nc.semaphore("setup_lam_ready"))
    stat = ctx.enter_context(nc.sbuf_tensor("setup_stat", [P, NT, 6], F32))
    mv = ctx.enter_context(nc.sbuf_tensor("setup_mv", [P, NT, 2], F32))
    tiny = ctx.enter_context(nc.sbuf_tensor("setup_tiny", [P, 64], F32))
    with nc.Block() as block:

        @block.sync
        def _(sp):
            for i in range(PARTS):
                sp.dma_start(g.x[:, i * W:(i + 1) * W, :], x_view[:, i * W:(i + 1) * W, :]).then_inc(x_loaded[i], 16)
            for out, in_ in late_loads:
                sp.dma_start(out, in_).then_inc(g.late_loaded, 16)

        @block.gpsimd
        def _(pool):
            pool.memset(g.minus_half[:], -0.5)
            pool.memset(g.three_halves[:], 1.5)
            pool.memset(g.euler[:], float(np.e))
            pool.memset(g.s_qs[:], 0.0)
            pool.memset(g.s_ks[:], 0.0)
            pool.memset(g.f_ss[:], 0.0)
            pool.memset(g.s_v1[:], 0.0).then_inc(zeroed, 1)
            pool.wait_ge(zeroed, 1)
            pool.memset(g.s_v1[:, :, :, :, 8:9], 1.0)

        @block.scalar
        def _(act):
            for out, in_ in small_loads:
                act.dma_start(out, in_).then_inc(small_loaded, 16)
            act.wait_ge(var_ready, 1)
            act.activation(g.rstd[0][:], g.rstd[0][:], ACT.Sqrt).then_inc(dev_ready, 1)
            act.wait_ge(dots_ready, 1)
            act.activation(tiny[:, 2:4], tiny[:, 0:2], ACT.Exp).then_inc(lam_ready, 1)

        @block.vector
        def _(dve):
            count = [0]

            def step(ins):
                count[0] += 1
                ins.then_inc(dve_step, 1)
                dve.wait_ge(dve_step, count[0])

            for i in range(PARTS):
                dve.wait_ge(x_loaded[i], 16)
                for t in range(i * W, (i + 1) * W):
                    ins = dve.bn_stats(stat[:, t, :], g.x[:, t, :])
            step(ins)
            for t in range(NT):
                ins = dve.bn_aggr(mv[:, t, :], stat[:, t, :])
            step(ins)
            dve.tensor_scalar(g.rstd[0][:], mv[:, :, 1], LN_EPS, None, ALU.add).then_inc(var_ready, 1)
            dve.tensor_copy(g.mean[0][:], mv[:, :, 0])
            dve.wait_ge(small_loaded, 16 * len(small_loads))
            step(dve.tensor_tensor(tiny[:, 24:40].rearrange("p (a b) -> p a b", a=2),
                                   g.lam_in[:, 0:2, :], g.lam_in[:, 2:4, :], ALU.mult))
            dve.tensor_reduce(tiny[:, 0:2], tiny[:, 24:40].rearrange("p (a b) -> p a b", a=2),
                              AX.X, ALU.add).then_inc(dots_ready, 1)
            step(dve.tensor_tensor(tiny[:, 8:16], g.qk_w[:, 0, :], g.qk_w[:, 1, :], ALU.mult))
            step(dve.tensor_scalar(g.qk_scale[:].rearrange("p (h d) -> p h d", d=HD),
                                   bc(tiny[:, 8:16].unsqueeze(1), [P, HEADS, HD]), SCALE, None, ALU.mult))
            step(dve.tensor_reduce(tiny[:, 16:17], tiny[:, 8:16], AX.X, ALU.max, apply_absolute_value=True))
            step(dve.tensor_scalar(g.minus_bound[:], tiny[:, 16:17], -HD * SCALE, None, ALU.mult))
            dve.wait_ge(lam_ready, 1)
            step(dve.tensor_tensor(tiny[:, 4:5], tiny[:, 3:4], tiny[:, 2:3], ALU.subtract))
            step(dve.tensor_scalar(g.minus_lam[:], tiny[:, 4:5], -LAMBDA_INIT, None, ALU.add))
            dve.wait_ge(dev_ready, 1)
            step(dve.reciprocal(g.rstd[0][:], g.rstd[0][:]))


STAGE = {"norm": 3, "xb": 3, "xt": 2, "qkv": 2, "xt_sb": 2, "qkv_sb": 2, "square": 2, "sums": 2, "newton": 2,
         "rot": 2, "operands": 2, "lo": 2, "v": 1, "kt": 1, "qp": 1, "kt_sb": 1, "qp_sb": 1, "max": 1,
         "max_sb": 1, "qf": 1, "qf_sb": 1, "otr": -1, "atr": -1, "pj": -1, "tokens": -1, "sq2": -1, "mean": -1,
         "pow": -1, "head": -1, "at_sb": -1, "residual": -1, "rstd": -1}
AT_A = {
    "pv": 7, "kt": (4, 6), "qp": (7, 9), "xt": (2,), "qkv": (3, 5), "otr": (3, 7), "atr": (11,), "pj": (14,),
    "kt_sb": (3, 5), "xt_sb": (2,), "square": (6,), "at_sb": (11,), "qp_sb": (7, 12), "norm": (10,),
    "v": (10,), "qkv_sb": (4, 4), "sums": (7,), "operands": (15,), "tokens": (6, 8), "residual": (12,),
    "newton": (8,), "lo": (11,), "xb": (15,), "rstd": (12,),
}
AT_B = {
    "pv": 6, "kt": (0, 1), "qp": (2, 5), "qf": (12, 14), "xt": (0,), "qkv": (1, 4), "otr": (3, 9),
    "atr": (14,), "pj": (15,), "max": (3, 4, 4, 5, 6, 7, 8, 9, 9, 10, 10, 10, 11, 13, 13, 13),
    "kt_sb": (0, 1), "qp_sb": (2, 4), "qf_sb": (13, 14), "xt_sb": (0,), "v": (2,), "qkv_sb": (1, 7),
    "at_sb": (13,), "norm": (1,), "operands": (15,), "tokens": (2, 9), "mean": (11,), "head": (14,),
    "residual": (15,), "max_sb": (3, 4, 4, 5, 6, 7, 8, 9, 9, 10, 10, 10, 11, 13, 13, 13), "rot": (0,),
    "sq2": (1,), "pow": (8,), "lo": (9,), "rstd": (15,),
}


def attention(nc, ctx, g, tag, psum):
    a, b = tag == "a", tag == "b"
    AT = AT_A if a else AT_B
    VW = 8 if a else 16
    NB = 4 if a else 2
    EH = 2 if a else 1
    NEX = HEADS // EH
    mean, rstd = (g.mean[0], g.rstd[0]) if a else (g.mean[2], g.rstd[2])
    mean_next, rstd_next = (g.mean[1], g.rstd[1]) if a else (g.mean[3], g.rstd[3])
    wqkv, wout = (g.wqkv_a, g.wproj) if a else (g.wqkv_b, g.wo)
    X2 = g.x[:, :, :].rearrange("p (n c) d -> p n (c d)", c=2)

    def ev(name, per):
        return Events(ctx, nc, f"{tag}_{name}", per)

    xn, xt = g.s_xn, g.s_xt
    qkv, qh = g.s_qkv, g.s_qh
    qs, ks, v1 = g.s_qs, g.s_ks, g.s_v1
    kt, qt, qp = g.s_kt, g.s_qt, g.s_qp
    probs, ot, an, at = g.s_probs, g.s_ot, g.s_an, g.s_at
    sq, ss, vh, y, yt = g.s_sq, g.s_ss, g.s_vh, g.s_y, g.s_yt
    rs, tv, a2 = g.s_rs, g.s_tv, g.s_a2

    def bank(i):
        return psum[:, 512 * i:512 * i + 512]

    PV = bank(NB)[:, 0:SEQ]
    M = [bank(3), bank(4)]
    QK = bank(5)
    XB = bank(6)
    OB = bank(7)

    filled = ev("filled", 1)
    xn_sb, xt_mm, xt_sb = ev("xn_sb", 2), ev("xt_mm", 1), ev("xt_sb", 1)
    xb_sb = ev("xb_sb", 1)
    qkv_mm, qkv_sb, v_sb = ev("qkv_mm", 2), ev("qkv_sb", 2), ev("v_sb", 1)
    sq_sb, ss_sb, seed, newton = ev("sq_sb", 1), ev("ss_sb", 1), ev("seed", 4), ev("newton", 12)
    rot, qh_sb, hi_sb, lo_sb = ev("rot", 2), ev("qh_sb", 2 if a else 1), ev("hi_sb", 2), ev("lo_sb", 2)
    kt_mm, kt_sb, qp_mm, qp_sb = ev("kt_mm", 2), ev("kt_sb", 2), ev("qp_mm", 2), ev("qp_sb", 2)
    mx_mm, mx_sb, qf_mm, qf_sb = ev("mx_mm", UNITS), ev("mx_sb", UNITS), ev("qf_mm", 2), ev("qf_sb", 2)
    s_mm, ex_sb, pv_mm, ot_sb = ev("s_mm", HEADS), ev("ex_sb", NEX), ev("pv_mm", 4), ev("ot_sb", 4)
    otr_mm, otr_used = ev("otr_mm", 2), ev("otr_used", 2)
    rs_sb, tv_sb, a2_sb = ev("rs_sb", 2 if a else 4), ev("tv_sb", 2), ev("a2_sb", 2)
    sq2_sb, ms_sb, var_sb, inv2_sb = ev("sq2_sb", 1), ev("ms_sb", 1), ev("var_sb", 1), ev("inv2_sb", 1)
    an_sb, atr_mm, at_sb, pj_mm, x_sb = ev("an_sb", 2), ev("atr_mm", 1), ev("at_sb", 1), ev("pj_mm", 1), ev("x_sb", 1)
    bn_sb, mv_sb, vare_sb, rstd_sb = ev("bn_sb", 1), ev("mv_sb", 1), ev("vare_sb", 1), ev("rstd_sb", 1)
    an_ready = otr_used if a else an_sb
    w_hi_sb = ev("w_hi_sb", 2)
    q_ready = qp_sb if a else qf_sb

    def march(eng, body):
        for n in (-3, -2, -1, 0, 1):
            body(Step(None, 0, n), n)
        with eng.Fori(0, 5) as i:
            body(Step(i, 2, 2), 2)
            body(Step(i, 2, 3), 3)
        for n in (12, 13, 14, 15, 16):
            body(Step(None, 0, n), n)

    def due(task, part, h, k):
        return [STAGE[task] - late for late in (0, 1)
                if AT[task][part] == h + HEADS * late and 0 <= k + STAGE[task] - late < NSEQ]

    with nc.Block() as block:

        @block.tensor
        def _(pe):
            def turn(dst, src):
                for q in range(4):
                    ins = pe.transpose(dst[:, q * P:(q + 1) * P], src[:, q * P:(q + 1) * P], g.identity[:])
                return ins

            def body(n, k):
                att, out = 0 <= k < NSEQ, 0 <= k - 1 < NSEQ

                def scores(h):
                    if h == 0:
                        pe.wait_ge(kt_sb.sem, kt_sb.upto(n))
                        pe.wait_ge(q_ready.sem, q_ready.upto(n))
                    if h >= NB:
                        pe.wait_ge(ex_sb.sem, ex_sb.upto(n, (h - NB) // EH + 1))
                    else:
                        pe.wait_ge(ex_sb.sem, ex_sb.upto(n - 1, (HEADS + h - NB) // EH + 1))
                    q, r, o = h // 4, 32 * (h % 4), h % NB
                    for c in range(2):
                        ins = pe.matmul(bank(o)[:, c * SEQ:(c + 1) * SEQ], kt[r:r + 32, k % 2, q, c * P:(c + 1) * P],
                                        qt[r:r + 32, k % 2, q, :], start=True, stop=True)
                    ins.then_inc(s_mm.sem, 1)

                def values(m, km, q):
                    if q == 0:
                        pe.wait_ge(v_sb.sem, v_sb.upto(m))
                    pe.wait_ge(ex_sb.sem, ex_sb.upto(m, (4 * q + 4) // EH))
                    pe.wait_ge(ot_sb.sem, ot_sb.upto(m, q))
                    for c in range(2):
                        for j in range(4):
                            h = 4 * q + j
                            ins = pe.matmul(PV[32 * j:32 * j + 32, :], v1[:, km % 2, c, h if a else h // 2, :],
                                            probs[:, h % 8, c, :], start=(c == 0), stop=(c == 1))
                    ins.then_inc(pv_mm.sem, 1)

                def k_turn(m, km, c):
                    pe.wait_ge(lo_sb.sem, lo_sb.upto(m))
                    if c == 0:
                        pe.wait_ge(q_ready.sem, q_ready.upto(m - 1))
                    else:
                        pe.wait_ge(kt_sb.sem, kt_sb.upto(m, 1))
                    turn(QK, ks[:, km % 2, c]).then_inc(kt_mm.sem, 1)

                def q_turn(m, km, c):
                    if c == 0:
                        pe.wait_ge(kt_sb.sem, kt_sb.upto(m))
                    else:
                        pe.wait_ge(qp_sb.sem, qp_sb.upto(m, 1))
                    turn(QK, qs[:, km % 2, c]).then_inc(qp_mm.sem, 1)

                def q_final(m, km, c):
                    pe.wait_ge(mx_sb.sem, mx_sb.upto(m, 8 * c + 8))
                    if c == 0:
                        pe.wait_ge(qp_sb.sem, qp_sb.upto(m))
                    else:
                        pe.wait_ge(qf_sb.sem, qf_sb.upto(m, 1))
                    turn(QK, qs[:, km % 2, c]).then_inc(qf_mm.sem, 1)

                def maxima(m, km, u):
                    c, v = u // 8, u % 8
                    r, pair = 32 * (v % 4), v // 4
                    pe.wait_ge(kt_sb.sem, kt_sb.upto(m))
                    pe.wait_ge(qp_sb.sem, qp_sb.upto(m, c + 1))
                    pe.wait_ge(mx_sb.sem, mx_sb.upto(m, u - 1))
                    for j in range(2):
                        q = 2 * pair + j
                        ins = pe.matmul(M[u % 2][:, j * SEQ:(j + 1) * SEQ], qp[r:r + 24, q, c * P:(c + 1) * P],
                                        kt[r:r + 24, km % 2, q, :], start=True, stop=True)
                    ins.then_inc(mx_mm.sem, 1)

                def x_turn(m, km):
                    pe.wait_ge(xn_sb.sem, xn_sb.upto(m))
                    pe.wait_ge(qkv_sb.sem, qkv_sb.upto(m - 1))
                    for c in range(2):
                        ins = pe.transpose(XB[:, c * P:(c + 1) * P], xn[:, km % 2, c, :], g.identity[:])
                    ins.then_inc(xt_mm.sem, 1)

                def project(m, km, c):
                    pe.wait_ge(xt_sb.sem, xt_sb.upto(m))
                    pe.wait_ge(qkv_sb.sem, qkv_sb.upto(m, c))
                    pe.matmul(XB[:, 0:3 * P], xt[:, c * P:(c + 1) * P], wqkv[:],
                              start=True, stop=True).then_inc(qkv_mm.sem, 1)

                def o_turn(m, km, c):
                    pe.wait_ge(ot_sb.sem, ot_sb.upto(m))
                    pe.wait_ge(x_sb.sem, x_sb.upto(m - 1))
                    pe.wait_ge(otr_used.sem, otr_used.upto(m, c))
                    for q in range(4):
                        ins = pe.transpose(OB[:, q * P:(q + 1) * P], ot[:, km % 2, q, c * P:(c + 1) * P],
                                           g.identity[:])
                    ins.then_inc(otr_mm.sem, 1)

                def a_turn(m, km):
                    pe.wait_ge(otr_used.sem, otr_used.upto(m))
                    pe.wait_ge(an_ready.sem, an_ready.upto(m))
                    for c in range(2):
                        ins = pe.transpose(OB[:, c * P:(c + 1) * P], an[:, c, :], g.identity[:])
                    ins.then_inc(atr_mm.sem, 1)

                def out_project(m, km):
                    pe.wait_ge(at_sb.sem, at_sb.upto(m))
                    for c in range(2):
                        ins = pe.matmul(OB[:, c * P:(c + 1) * P], at[:, c * P:(c + 1) * P], wout[:],
                                        start=True, stop=True)
                    ins.then_inc(pj_mm.sem, 1)

                for h in range(HEADS):
                    if att:
                        scores(h)
                    for q in range(4):
                        if out and 4 * q + AT["pv"] == h + HEADS:
                            values(n - 1, k - 1, q)
                        if att and 4 * q + AT["pv"] == h:
                            values(n, k, q)
                    for c in range(2):
                        for off in due("kt", c, h, k):
                            k_turn(n + off, k + off, c)
                        for off in due("qp", c, h, k):
                            q_turn(n + off, k + off, c)
                    for off in due("xt", 0, h, k):
                        x_turn(n + off, k + off)
                    for c in range(2):
                        for off in due("qkv", c, h, k):
                            project(n + off, k + off, c)
                        for off in due("otr", c, h, k):
                            o_turn(n + off, k + off, c)
                    for off in due("atr", 0, h, k):
                        a_turn(n + off, k + off)
                    for off in due("pj", 0, h, k):
                        out_project(n + off, k + off)
                    for u in range(UNITS if b else 0):
                        for off in due("max", u, h, k):
                            maxima(n + off, k + off, u)
                    for c in range(2 if b else 0):
                        for off in due("qf", c, h, k):
                            q_final(n + off, k + off, c)

            march(pe, body)

        @block.scalar
        def _(act):
            def four(ap):
                return ap.rearrange("p (q t) -> p q t", q=4)

            def body(n, k):
                att, out = 0 <= k < NSEQ, 0 <= k - 1 < NSEQ

                def exps(h):
                    act.wait_ge(s_mm.sem, s_mm.upto(n, h + 1))
                    first = h - EH + 1
                    if first >= 8:
                        act.wait_ge(pv_mm.sem, pv_mm.upto(n, (first - 8) // 4 + 1))
                    else:
                        act.wait_ge(pv_mm.sem, pv_mm.upto(n - 1, first // 4 + 3))
                    dst = probs[:, first % 8:first % 8 + EH, :, :].rearrange("p j c s -> p (j c s)")
                    src = psum[:, first % NB * 512:(first % NB + EH) * 512]
                    act.activation(dst, src, ACT.Exp,
                                   bias=g.minus_bound[:] if a else 0.0).then_inc(ex_sb.sem, 1)

                def o_keep(m, km, q):
                    act.wait_ge(pv_mm.sem, pv_mm.upto(m, q + 1))
                    if q == 0:
                        act.wait_ge(otr_mm.sem, otr_mm.upto(m - 2))
                    act.activation(ot[:, km % 2, q, :], PV, ACT.Copy).then_inc(ot_sb.sem, 1)

                for h in range(HEADS):
                    if att and h % EH == EH - 1:
                        exps(h)
                    if b:
                        for q in range(4):
                            if out and 4 * q + AT["pv"] == h + HEADS:
                                o_keep(n - 1, k - 1, q)
                            if att and 4 * q + AT["pv"] == h:
                                o_keep(n, k, q)
                    for c in range(2):
                        for off in due("kt_sb", c, h, k):
                            m, km = n + off, k + off
                            act.wait_ge(kt_mm.sem, kt_mm.upto(m, c + 1))
                            act.activation(kt[:, km % 2, :, c * P:(c + 1) * P], four(QK),
                                           ACT.Copy).then_inc(kt_sb.sem, 1)
                        for off in due("qp_sb", c, h, k) if b else ():
                            m, km = n + off, k + off
                            act.wait_ge(qp_mm.sem, qp_mm.upto(m, c + 1))
                            act.wait_ge(mx_mm.sem, mx_mm.upto(m - 1))
                            act.activation(qp[:, :, c * P:(c + 1) * P], four(QK),
                                           ACT.Copy).then_inc(qp_sb.sem, 1)
                        for off in due("qf_sb", c, h, k) if b else ():
                            m, km = n + off, k + off
                            act.wait_ge(qf_mm.sem, qf_mm.upto(m, c + 1))
                            act.activation(qt[:, km % 2, :, c * P:(c + 1) * P], four(QK),
                                           ACT.Copy).then_inc(qf_sb.sem, 1)
                    for off in due("xt_sb", 0, h, k):
                        m, km = n + off, k + off
                        act.wait_ge(xt_mm.sem, xt_mm.upto(m))
                        act.wait_ge(qkv_mm.sem, qkv_mm.upto(m - 1))
                        act.activation(xt[:], XB[:, 0:SEQ], ACT.Copy).then_inc(xt_sb.sem, 1)
                    for off in due("v", 0, h, k) if b else ():
                        m, km = n + off, k + off
                        act.wait_ge(pv_mm.sem, pv_mm.upto(m - 2))
                        act.wait_ge(qkv_sb.sem, qkv_sb.upto(m))
                        act.activation(v1[:, km % 2, :, 0:8, 0:VW],
                                       qkv[:, km % 2, 2, :, :].rearrange("p c (h d) -> p c h d", d=VW),
                                       ACT.Copy).then_inc(v_sb.sem, 1)
                    for c in range(2):
                        for off in due("qkv_sb", c, h, k) if b else ():
                            m, km = n + off, k + off
                            act.wait_ge(qkv_mm.sem, qkv_mm.upto(m, c + 1))
                            act.wait_ge(v_sb.sem, v_sb.upto(m - 2))
                            act.wait_ge(rot.sem, rot.upto(m - 2))
                            act.activation(qkv[:, km % 2, :, c, :],
                                           XB[:, 0:3 * P].rearrange("p (a d) -> p a d", a=3),
                                           ACT.Copy).then_inc(qkv_sb.sem, 1)
                    for off in due("square", 0, h, k) if a else ():
                        m, km = n + off, k + off
                        act.wait_ge(qkv_sb.sem, qkv_sb.upto(m))
                        act.wait_ge(ss_sb.sem, ss_sb.upto(m - 1))
                        act.activation(sq[:], qkv[:, km % 2, 0:2, :, :].rearrange("p a c d -> p (a c d)"),
                                       ACT.Square).then_inc(sq_sb.sem, 1)
                    for off in due("at_sb", 0, h, k):
                        m, km = n + off, k + off
                        act.wait_ge(atr_mm.sem, atr_mm.upto(m))
                        act.activation(at[:], OB[:, 0:SEQ], ACT.Copy).then_inc(at_sb.sem, 1)

            march(act, body)

        @block.gpsimd
        def _(pool):
            def body(n, k):
                if a and k in (13, 14):
                    pool.wait_ge(g.late_loaded, g.late_count)
                    pool.wait_ge(w_hi_sb.sem, k - 12)
                    w, hi, lo = ((g.w1, g.w1_hi, g.w1_lo), (g.w3, g.w3_hi, g.w3_lo))[k - 13]
                    pool.tensor_tensor(lo[:], w[:], hi[:], ALU.subtract)
                for h in range(HEADS):
                    for off in due("xb", 0, h, k) if a else ():
                        m = n + off
                        pool.wait_ge(xn_sb.sem, xn_sb.upto(m))
                        pool.tensor_tensor(X2[:, m.at, :].rearrange("p (c d) -> p c d", c=2),
                                           X2[:, m.at, :].rearrange("p (c d) -> p c d", c=2),
                                           bc(g.bproj[:].unsqueeze(1), [P, 2, DIM]), ALU.add).then_inc(xb_sb.sem, 1)
                    for off in due("rot", 0, h, k) if b else ():
                        m, km = n + off, k + off
                        pool.wait_ge(qkv_sb.sem, qkv_sb.upto(m))
                        pool.wait_ge(qh_sb.sem, qh_sb.upto(m - 1))
                        flat = qkv[:, km % 2, 0:2, :, :].rearrange("p a c d -> p (a c d)")
                        pool.tensor_tensor(g.s_rot[:, 0, :], flat, g.rope_cos[:], ALU.mult).then_inc(rot.sem, 1)
                        pool.tensor_tensor(g.s_rot[:, 1, :].rearrange("p (i e) -> p i e", e=2),
                                           flat.rearrange("p (i e) -> p i e", e=2)[:, :, ::-1],
                                           g.rope_sin[:].rearrange("p (i e) -> p i e", e=2),
                                           ALU.mult).then_inc(rot.sem, 1)
                    for off in due("newton", 0, h, k) if a else ():
                        m = n + off
                        pool.wait_ge(seed.sem, seed.upto(m))
                        i = 0
                        for _ in range(3):
                            for o, u, w, op in ((yt, y, y, ALU.mult), (yt, yt, vh, ALU.mult),
                                                (yt, yt, g.three_halves, ALU.add), (y, y, yt, ALU.mult)):
                                if i:
                                    pool.wait_ge(newton.sem, newton.upto(m, i))
                                pool.tensor_tensor(o[:], u[:], w[:], op).then_inc(newton.sem, 1)
                                i += 1
                    for off in due("lo", 0, h, k):
                        m, km = n + off, k + off
                        for i, dst in enumerate((qs, ks)):
                            pool.wait_ge(hi_sb.sem, hi_sb.upto(m, i + 1))
                            d4 = dst[:, km % 2, :, :].rearrange("p c (h s d) -> p (c h) s d", s=4, d=HD)
                            pool.tensor_tensor(d4[:, :, 2 if i == 0 else 1, :],
                                               qh[:, i, :].rearrange("p (h d) -> p h d", d=HD),
                                               d4[:, :, 0, :], ALU.subtract).then_inc(lo_sb.sem, 1)
                    for off in due("sq2", 0, h, k) if b else ():
                        m = n + off
                        pool.wait_ge(a2_sb.sem, a2_sb.upto(m))
                        flat = a2[:, :, :].rearrange("p c d -> p (c d)")
                        pool.tensor_tensor(g.s_sq2[:], flat, flat, ALU.mult).then_inc(sq2_sb.sem, 1)
                    for off in due("pow", 0, h, k) if b else ():
                        m = n + off
                        pool.wait_ge(var_sb.sem, var_sb.upto(m))
                        pool.tensor_tensor(g.s_inv2[:], g.s_var2[:], g.minus_half[:, 0:16],
                                           ALU.pow).then_inc(inv2_sb.sem, 1)
                    for off in due("rstd", 0, h, k):
                        m = n + off
                        pool.wait_ge(vare_sb.sem, vare_sb.upto(m))
                        pool.tensor_tensor(rstd_next[:, :].rearrange("p (n c) -> p n c", c=2)[:, m.at, :],
                                           g.s_vare[:], g.minus_half[:, 0:2], ALU.pow).then_inc(rstd_sb.sem, 1)

            march(pool, body)

        @block.vector
        def _(dve):
            if b:
                dve.memset(v1[:, :, :, :, VW:VW + 1], 1.0).then_inc(filled.sem, 1)
                dve.memset(ks[:].rearrange("p r c (h s) -> p (r c h) s", s=32)[:, :, 24:25],
                           1.0).then_inc(filled.sem, 1)
                dve.wait_ge(filled.sem, 2)

            def body(n, k):
                att, out = 0 <= k < NSEQ, 0 <= k - 1 < NSEQ

                def normalise(m, km):
                    dve.wait_ge(xt_mm.sem, xt_mm.upto(m - 2))
                    for c in range(2):
                        dve.tensor_scalar(xn[:, km % 2, c, :], g.x[:, ((m) * 2 + c).at, :],
                                          pair_of(mean, m, c), pair_of(rstd, m, c),
                                          ALU.subtract, ALU.mult).then_inc(xn_sb.sem, 1)

                def split(m, km, i, dst):
                    d4 = dst[:, km % 2, :, :].rearrange("p c (h s d) -> p (c h) s d", s=4, d=HD)
                    o = d4[:, :, 0:2, :] if i == 0 else d4[:, :, 0:3:2, :]
                    src = qh[:, i, :].rearrange("p (h d) -> p h d", d=HD).unsqueeze(2)
                    dve.tensor_copy(o.bitcast(F32R), bc(src, [P, 32, 2, HD])).then_inc(hi_sb.sem, 1)

                def operands(m, km):
                    q_seen = qp_mm if a else qf_mm
                    dve.wait_ge(q_seen.sem, q_seen.upto(m - 2))
                    dve.wait_ge(kt_mm.sem, kt_mm.upto(m - 2))
                    dve.wait_ge(lo_sb.sem, lo_sb.upto(m - 1))
                    if a:
                        dve.wait_ge(newton.sem, newton.upto(m))
                        flat = qkv[:, km % 2, 0:2, :, :].rearrange("p a c (h d) -> p (a c h) d", d=HD)
                        dve.tensor_tensor(qh[:].rearrange("p a (h d) -> p (a h) d", d=HD), flat,
                                          bc(y[:].unsqueeze(2), [P, 64, HD]), ALU.mult).then_inc(qh_sb.sem, 1)
                        dve.wait_ge(qh_sb.sem, qh_sb.upto(m, 1))
                        qc = qh[:, 0, :].rearrange("p (c d) -> p c d", c=2)
                        dve.tensor_tensor(qc, qc, bc(g.qk_scale[:].unsqueeze(1), [P, 2, DIM]),
                                          ALU.mult).then_inc(qh_sb.sem, 1)
                    else:
                        dve.wait_ge(rot.sem, rot.upto(m))
                        dve.tensor_tensor(qh[:].rearrange("p a d -> p (a d)"), g.s_rot[:, 0, :],
                                          g.s_rot[:, 1, :], ALU.add).then_inc(qh_sb.sem, 1)
                    dve.wait_ge(qh_sb.sem, qh_sb.upto(m))
                    split(m, km, 0, qs)
                    split(m, km, 1, ks)

                def first_guess(m):
                    dve.wait_ge(sq_sb.sem, sq_sb.upto(m))
                    dve.wait_ge(newton.sem, newton.upto(m - 1))
                    dve.wait_ge(qh_sb.sem, qh_sb.upto(m - 1))
                    dve.tensor_reduce(ss[:], sq[:].rearrange("p (h d) -> p h d", d=HD),
                                      AX.X, ALU.add).then_inc(ss_sb.sem, 1)
                    dve.wait_ge(ss_sb.sem, ss_sb.upto(m))
                    dve.tensor_scalar(g.s_v[:], ss[:], 1.0 / HD, RMS_EPS_A, ALU.mult, ALU.add
                                      ).then_inc(seed.sem, 1)
                    dve.wait_ge(seed.sem, seed.upto(m, 1))
                    dve.tensor_scalar(vh[:], g.s_v[:], -0.5, None, ALU.mult).then_inc(seed.sem, 1)
                    dve.tensor_scalar(g.s_i[:], g.s_v[:].bitcast(I32), 1, None,
                                      ALU.logical_shift_right).then_inc(seed.sem, 1)
                    dve.wait_ge(seed.sem, seed.upto(m, 3))
                    dve.tensor_scalar(y[:].bitcast(I32), g.s_i[:], -1.0, float(0x5F3759DF),
                                      ALU.mult, ALU.add).then_inc(seed.sem, 1)

                def tokens(m, km, c):
                    dve.wait_ge(otr_mm.sem, otr_mm.upto(m, c + 1))
                    o3 = OB.rearrange("p (h s) -> p h s", s=32)
                    dve.reciprocal(rs[:].unsqueeze(2), o3[:, :, VW:VW + 1]).then_inc(rs_sb.sem, 1)
                    if a:
                        dve.wait_ge(rs_sb.sem, rs_sb.upto(m, c + 1))
                        dve.wait_ge(atr_mm.sem, atr_mm.upto(m - 1))
                        dve.tensor_tensor(an[:, c, :].rearrange("p (h d) -> p h d", d=HD), o3[:, :, 0:VW],
                                          bc(rs[:].unsqueeze(2), [P, HEADS, VW]),
                                          ALU.mult).then_inc(otr_used.sem, 1)
                        return
                    dve.wait_ge(rs_sb.sem, rs_sb.upto(m, 2 * c + 1))
                    odd = rs[:].rearrange("p (h e) -> p h e", e=2)[:, :, 1:2]
                    dve.tensor_scalar(odd, odd, g.minus_lam[:], None, ALU.mult).then_inc(rs_sb.sem, 1)
                    dve.wait_ge(rs_sb.sem, rs_sb.upto(m, 2 * c + 2))
                    dve.tensor_tensor(tv[:].rearrange("p (h d) -> p h d", d=VW), o3[:, :, 0:VW],
                                      bc(rs[:].unsqueeze(2), [P, HEADS, VW]), ALU.mult).then_inc(otr_used.sem, 1)
                    dve.wait_ge(otr_used.sem, otr_used.upto(m, c + 1))
                    t4 = tv[:].rearrange("p (h e d) -> p h e d", e=2, d=VW)
                    dve.wait_ge(sq2_sb.sem, sq2_sb.upto(m - 1))
                    dve.wait_ge(an_sb.sem, an_sb.upto(m - 1))
                    dve.tensor_tensor(a2[:, c, :].rearrange("p (h d) -> p h d", d=VW),
                                      t4[:, :, 0, :], t4[:, :, 1, :], ALU.add).then_inc(a2_sb.sem, 1)

                def mean_square(m):
                    dve.wait_ge(sq2_sb.sem, sq2_sb.upto(m))
                    dve.tensor_reduce(g.s_ms2[:], g.s_sq2[:].rearrange("p (h d) -> p h d", d=16),
                                      AX.X, ALU.add).then_inc(ms_sb.sem, 1)
                    dve.wait_ge(ms_sb.sem, ms_sb.upto(m))
                    dve.tensor_scalar(g.s_var2[:], g.s_ms2[:], 1.0 / 16, RMS_EPS_B,
                                      ALU.mult, ALU.add).then_inc(var_sb.sem, 1)

                def head_norm(m):
                    dve.wait_ge(inv2_sb.sem, inv2_sb.upto(m))
                    dve.wait_ge(atr_mm.sem, atr_mm.upto(m - 1))
                    for c in range(2):
                        dve.scalar_tensor_tensor(
                            out=an[:, c, :].rearrange("p (h d) -> p h d", d=16),
                            in0=a2[:, c, :].rearrange("p (h d) -> p h d", d=16), scalar=1.0 - LAMBDA_INIT,
                            in1=bc(g.s_inv2[:, 8 * c:8 * c + 8].unsqueeze(2), [P, 8, 16]),
                            op0=ALU.mult, op1=ALU.mult).then_inc(an_sb.sem, 1)

                def residual(m):
                    dve.wait_ge(pj_mm.sem, pj_mm.upto(m))
                    if a:
                        dve.wait_ge(xb_sb.sem, xb_sb.upto(m))
                    dve.tensor_tensor(X2[:, (m).at, :], OB[:, 0:SEQ], X2[:, (m).at, :],
                                      ALU.add).then_inc(x_sb.sem, 1)
                    dve.wait_ge(x_sb.sem, x_sb.upto(m))
                    dve.wait_ge(rstd_sb.sem, rstd_sb.upto(m - 1))
                    dve.memset(g.s_pad[:, 3:4], 0.0)
                    for c in range(2):
                        ins = dve.bn_stats(g.s_bn[:, c, :], g.x[:, (m * 2 + c).at, :])
                    ins.then_inc(bn_sb.sem, 1)
                    dve.wait_ge(bn_sb.sem, bn_sb.upto(m))
                    dve.memset(g.s_pad[:, 3:4], 0.0)
                    for c in range(2):
                        ins = dve.bn_aggr(g.s_mv[:, c, :], g.s_bn[:, c, :])
                    ins.then_inc(mv_sb.sem, 1)
                    dve.wait_ge(mv_sb.sem, mv_sb.upto(m))
                    dve.tensor_scalar(g.s_vare[:], g.s_mv[:, 0:2, 1], LN_EPS, None, ALU.add).then_inc(vare_sb.sem, 1)
                    dve.tensor_copy(mean_next[:, :].rearrange("p (n c) -> p n c", c=2)[:, (m).at, :],
                                    g.s_mv[:, 0:2, 0])

                def o_keep(m, km, q):
                    dve.wait_ge(pv_mm.sem, pv_mm.upto(m, q + 1))
                    if q == 0:
                        dve.wait_ge(otr_mm.sem, otr_mm.upto(m - 2))
                    dve.tensor_copy(ot[:, km % 2, q, :], PV).then_inc(ot_sb.sem, 1)

                if a and k == 12:
                    dve.wait_ge(g.late_loaded, g.late_count)
                    dve.tensor_copy(g.w1_hi[:], g.w1[:]).then_inc(w_hi_sb.sem, 1)
                    dve.tensor_copy(g.w3_hi[:], g.w3[:]).then_inc(w_hi_sb.sem, 1)
                    dve.tensor_copy(g.select[:], g.select_raw[:])
                for h in range(HEADS):
                    for q in range(4 if a else 0):
                        if out and 4 * q + AT["pv"] == h + HEADS:
                            o_keep(n - 1, k - 1, q)
                        if att and 4 * q + AT["pv"] == h:
                            o_keep(n, k, q)
                    for off in due("norm", 0, h, k):
                        normalise(n + off, k + off)
                    for off in due("operands", 0, h, k):
                        operands(n + off, k + off)
                    for c in range(2):
                        for off in due("tokens", c, h, k):
                            tokens(n + off, k + off, c)
                        for off in due("qkv_sb", c, h, k) if a else ():
                            m, km = n + off, k + off
                            dve.wait_ge(qkv_mm.sem, qkv_mm.upto(m, c + 1))
                            dve.wait_ge(v_sb.sem, v_sb.upto(m - 2))
                            dve.wait_ge(qh_sb.sem, qh_sb.upto(m - 2))
                            dve.tensor_tensor(qkv[:, km % 2, :, c, :],
                                              XB[:, 0:3 * P].rearrange("p (a d) -> p a d", a=3),
                                              g.bqkv[:].rearrange("p (a d) -> p a d", a=3),
                                              ALU.add).then_inc(qkv_sb.sem, 1)
                        for off in due("qp_sb", c, h, k) if a else ():
                            m, km = n + off, k + off
                            dve.wait_ge(qp_mm.sem, qp_mm.upto(m, c + 1))
                            dve.tensor_copy(qt[:, km % 2, :, c * P:(c + 1) * P],
                                            QK.rearrange("p (q t) -> p q t", q=4)).then_inc(qp_sb.sem, 1)
                    for off in due("v", 0, h, k) if a else ():
                        m, km = n + off, k + off
                        dve.wait_ge(pv_mm.sem, pv_mm.upto(m - 2))
                        dve.tensor_copy(v1[:, km % 2, :, :, 0:VW],
                                        qkv[:, km % 2, 2, :, :].rearrange(
                                            "p c (h d) -> p c h d", d=VW)).then_inc(v_sb.sem, 1)
                    for off in due("sums", 0, h, k) if a else ():
                        first_guess(n + off)
                    for off in due("mean", 0, h, k) if b else ():
                        mean_square(n + off)
                    for off in due("head", 0, h, k) if b else ():
                        head_norm(n + off)
                    for off in due("residual", 0, h, k):
                        residual(n + off)
                    for u in range(UNITS if b else 0):
                        for off in due("max_sb", u, h, k):
                            m, km = n + off, k + off
                            c, v = u // 8, u % 8
                            o = qs[:, km % 2, c, :].rearrange("p (q r s) -> p q r s", q=4, r=4)
                            dve.wait_ge(mx_mm.sem, mx_mm.upto(m, u + 1))
                            dve.tensor_reduce(o[:, 2 * (v // 4):2 * (v // 4) + 2, v % 4, 24:25].bitcast(F32R),
                                              M[u % 2].rearrange("p (j s) -> p j s", j=2),
                                              AX.X, ALU.max, negate=True).then_inc(mx_sb.sem, 1)

            march(dve, body)


def pair_of(ap, n, c):
    return ap[:, :].rearrange("p (n c) -> p n c", c=2)[:, n.at, c:c + 1]


LOW_ON_DVE = (5, 6, 7)
FF = {"norm": 8, "x_turn": 0, "xt_sb": 0, "logits": 1, "best": 1, "pow": (2, 2, 3, 4), "gates": 5,
      "s_turn": 6, "st_sb": 6, "residual": 0, "rstd": 1}


def feed_forward(nc, ctx, g, tag, psum, out):
    first = tag == "f"
    mean, rstd = (g.mean[1], g.rstd[1]) if first else (g.mean[3], g.rstd[3])
    mean_next, rstd_next = g.mean[2], g.rstd[2]
    X4 = g.x[:, :, :].rearrange("p (n c) d -> p n (c d)", c=4)
    xn, xt, st, ssp = g.f_xn, g.f_xt, g.f_st, g.f_ss
    xe, xe_hi, xe_lo = g.f_xe, g.f_xe_hi, g.f_xe_lo
    T, SB = psum[:, 0:512], psum[:, 512:1024]
    H1 = [psum[:, 1024:1536], psum[:, 1536:2048]]
    H3 = [psum[:, 2048:2560], psum[:, 2560:3072]]
    Y = [psum[:, 3072:3584], psum[:, 3584:4096]]
    NE = E + 1
    PIECES = 4

    def ev(name, per):
        return Events(ctx, nc, f"{tag}_{name}", per)

    xn_sb, xt_mm, xt_sb, lg_mm, lg_sb = ev("xn_sb", 4), ev("xt_mm", 1), ev("xt_sb", 1), ev("lg_mm", 1), ev("lg_sb", 1)
    top_sb, idx_sb, ix_sb, sh_sb, pw_sb = ev("top_sb", 1), ev("idx_sb", 1), ev("ix_sb", 1), ev("sh_sb", 1), ev("pw_sb", PIECES)
    gs_sb, m_sb, sc_sb, hi_sb, lo_sb = ev("gs_sb", 2), ev("m_sb", 3), ev("sc_sb", 2), ev("hi_sb", 1), ev("lo_sb", 1)
    st_mm, st_sb = ev("st_mm", 1), ev("st_sb", 1)
    sb_mm, xe_sb, xe_hi_sb = ev("sb_mm", E), ev("xe_sb", E), ev("xe_hi_sb", NE)
    xe_lo_pool, xe_lo_dve = ev("xe_lo_pool", NE - len(LOW_ON_DVE)), ev("xe_lo_dve", len(LOW_ON_DVE))
    h1_mm, h3_mm, g_sb, h_sb = ev("h1_mm", NE), ev("h3_mm", NE), ev("g_sb", NE), ev("h_sb", NE)
    y_mm, x_sb = ev("y_mm", NE), ev("x_sb", 1)
    bn_sb, mv_sb, vare_sb, rstd_sb = ev("bn_sb", 1), ev("mv_sb", 1), ev("vare_sb", 1), ev("rstd_sb", 1)
    stored = ctx.enter_context(nc.semaphore(f"{tag}_stored"))

    def march(eng, body):
        for n in (-1, 0, 1):
            body(Step(None, 0, n), n)
        with eng.Fori(0, 2) as i:
            body(Step(i, 2, 2), 2)
            body(Step(i, 2, 3), 3)
        for n in (6, 7, 8):
            body(Step(None, 0, n), n)

    def ahead(n, k, e, by):
        if e + by < NE:
            return [(n, k, e + by)] if 0 <= k < NCH else []
        return [(n + 1, k + 1, e + by - NE)] if 0 <= k + 1 < NCH else []

    def ring(e):
        return e % 4 if e < E else 4

    def low_of(e):
        on_dve = e in LOW_ON_DVE
        return (xe_lo_dve if on_dve else xe_lo_pool,
                sum((x in LOW_ON_DVE) == on_dve for x in range(e + 1)))

    with nc.Block() as block:

        @block.tensor
        def _(pe):
            def body(n, k):
                run, gate = 0 <= k < NCH, 0 <= k + 1 < NCH

                def spread(m, km, e):
                    if e == 0:
                        pe.wait_ge(st_sb.sem, st_sb.upto(m))
                        pe.wait_ge(xe_sb.sem, xe_sb.upto(m - 1))
                    else:
                        pe.wait_ge(xe_sb.sem, xe_sb.upto(m, e))
                    pe.matmul(SB, g.select[:, e, :], st[:, km % 2, :],
                              start=True, stop=True).then_inc(sb_mm.sem, 1)

                def thrice(dst, w_hi, w_lo, x_hi, x_lo):
                    pe.matmul(dst, w_hi, x_hi, start=True, stop=False)
                    pe.matmul(dst, w_lo, x_hi, start=False, stop=False)
                    return pe.matmul(dst, w_hi, x_lo, start=False, stop=True)

                def up(m, km, e):
                    low, j = low_of(e)
                    pe.wait_ge(low.sem, low.upto(m, j))
                    x_hi, x_lo = xe_hi[:, ring(e), :], xe_lo[:, ring(e), :]
                    q = (e + km) % 2
                    if e >= 2:
                        pe.wait_ge(g_sb.sem, g_sb.upto(m, e - 1))
                    elif km > 0:
                        pe.wait_ge(g_sb.sem, g_sb.upto(m - 1, 8 + e))
                    thrice(H1[q], g.w1_hi[:, e, :], g.w1_lo[:, e, :], x_hi, x_lo).then_inc(h1_mm.sem, 1)
                    if e >= 2:
                        pe.wait_ge(h_sb.sem, h_sb.upto(m, e - 1))
                    elif km > 0:
                        pe.wait_ge(h_sb.sem, h_sb.upto(m - 1, 8 + e))
                    thrice(H3[q], g.w3_hi[:, e, :], g.w3_lo[:, e, :], x_hi, x_lo).then_inc(h3_mm.sem, 1)

                def down(e):
                    pe.wait_ge(h_sb.sem, h_sb.upto(n, e + 1))
                    if e == 0:
                        pe.wait_ge(x_sb.sem, x_sb.upto(n - 2))
                    q = (e + k) % 2
                    for t in range(4):
                        ins = pe.matmul(Y[k % 2][:, t * P:(t + 1) * P], g.f_h[:, q, t * P:(t + 1) * P],
                                        g.w2[:, e, :], start=(e == 0 and t == 0), stop=(e == NE - 1 and t == 3),
                                        skip_group_check=True)
                    ins.then_inc(y_mm.sem, 1)

                def x_turn():
                    pe.wait_ge(xn_sb.sem, xn_sb.upto(n + 1))
                    pe.wait_ge(st_sb.sem, st_sb.upto(n))
                    for t in range(4):
                        ins = pe.transpose(T[:, t * P:(t + 1) * P], xn[:, t, :], g.identity[:])
                    ins.then_inc(xt_mm.sem, 1)

                def logits():
                    pe.wait_ge(xt_sb.sem, xt_sb.upto(n + 1))
                    for t in range(4):
                        ins = pe.matmul(T[:, t * E:(t + 1) * E], xt[:, (k + 1) % 2, t * P:(t + 1) * P], g.gate[:],
                                        start=True, stop=True)
                    ins.then_inc(lg_mm.sem, 1)

                def s_turn():
                    pe.wait_ge(lo_sb.sem, lo_sb.upto(n + 1))
                    for t in range(4):
                        ins = pe.transpose(T[:, t * P:(t + 1) * P], ssp[:, t, :], g.identity[:])
                    ins.then_inc(st_mm.sem, 1)

                for e in range(NE):
                    for m, km, next_e in ahead(n, k, e, 1):
                        up(m, km, next_e)
                    for m, km, next_e in ahead(n, k, e, 3):
                        if next_e not in (0, E):
                            spread(m, km, next_e)
                    if gate and e == FF["x_turn"]:
                        x_turn()
                    if gate and e == FF["logits"]:
                        logits()
                    if gate and e == FF["s_turn"]:
                        s_turn()
                    if run:
                        down(e)
                    for m, km, next_e in ahead(n, k, e, 3):
                        if next_e == 0:
                            spread(m, km, next_e)

            march(pe, body)

        @block.scalar
        def _(act):
            def body(n, k):
                run, gate = 0 <= k < NCH, 0 <= k + 1 < NCH

                def silu(m, km, e):
                    act.wait_ge(h1_mm.sem, h1_mm.upto(m, e + 1))
                    if e >= 2:
                        act.wait_ge(h_sb.sem, h_sb.upto(m, e - 1))
                    elif km > 0:
                        act.wait_ge(h_sb.sem, h_sb.upto(m - 1, 8 + e))
                    q = (e + km) % 2
                    act.activation(g.f_g[:, q, :], H1[q], ACT.Silu).then_inc(g_sb.sem, 1)

                def high(m, km, e):
                    if e < E:
                        act.wait_ge(xe_sb.sem, xe_sb.upto(m, e + 1))
                        src = xe[:, e % 2, :]
                    else:
                        act.wait_ge(xt_sb.sem, xt_sb.upto(m))
                        src = xt[:, km % 2, :]
                    if 4 <= e < E:
                        act.wait_ge(h3_mm.sem, h3_mm.upto(m, e - 3))
                    elif km > 0:
                        act.wait_ge(h3_mm.sem, h3_mm.upto(m - 1, e + 5 if e < E else NE))
                    act.activation(xe_hi[:, ring(e), :], src, ACT.Copy).then_inc(xe_hi_sb.sem, 1)

                for e in range(NE):
                    for m, km, next_e in ahead(n, k, e, 1):
                        silu(m, km, next_e)
                    if gate and e == FF["st_sb"]:
                        act.wait_ge(st_mm.sem, st_mm.upto(n + 1))
                        act.activation(st[:, (k + 1) % 2, :], T, ACT.Copy).then_inc(st_sb.sem, 1)
                    for m, km, next_e in ahead(n, k, e, 3):
                        high(m, km, next_e)
                    if gate and e == FF["xt_sb"]:
                        act.wait_ge(xt_mm.sem, xt_mm.upto(n + 1))
                        if k > 0:
                            act.wait_ge(xe_lo_pool.sem, xe_lo_pool.upto(n - 1))
                        act.activation(xt[:, (k + 1) % 2, :], T, ACT.Copy).then_inc(xt_sb.sem, 1)

            march(act, body)

        @block.gpsimd
        def _(pool):
            def body(n, k):
                gate = 0 <= k + 1 < NCH

                def low(m, km, e):
                    src = xe[:, e % 2, :] if e < E else xt[:, km % 2, :]
                    pool.wait_ge(xe_hi_sb.sem, xe_hi_sb.upto(m, e + 1))
                    pool.tensor_tensor(xe_lo[:, ring(e), :], src, xe_hi[:, ring(e), :],
                                       ALU.subtract).then_inc(xe_lo_pool.sem, 1)

                for e in range(NE):
                    for i in range(PIECES):
                        if gate and e == FF["pow"][i]:
                            if i == 0:
                                pool.wait_ge(sh_sb.sem, sh_sb.upto(n + 1))
                            w = 4 * E // PIECES
                            pool.tensor_tensor(g.f_p[:, i * w:(i + 1) * w], g.euler[:, 0:w],
                                               g.f_sh[:, i * w:(i + 1) * w], ALU.pow).then_inc(pw_sb.sem, 1)
                    for m, km, next_e in ahead(n, k, e, 3):
                        if next_e not in LOW_ON_DVE:
                            low(m, km, next_e)
                    if first and 0 <= k - 1 < NCH and e == FF["rstd"]:
                        pool.wait_ge(vare_sb.sem, vare_sb.upto(n - 1))
                        pool.tensor_tensor(
                            rstd_next[:, :].rearrange("p (n c) -> p n c", c=4)[:, (n - 1).at, :], g.f_vare[:],
                            g.minus_half[:, 0:4], ALU.pow).then_inc(rstd_sb.sem, 1)

            march(pool, body)

        @block.vector
        def _(dve):
            def body(n, k):
                run, gate = 0 <= k < NCH, 0 <= k + 1 < NCH

                def scale(m, km, e):
                    dve.wait_ge(sb_mm.sem, sb_mm.upto(m, e + 1))
                    if e >= 2:
                        low, j = low_of(e - 2)
                        dve.wait_ge(low.sem, low.upto(m, j))
                    elif km > 0:
                        low, j = low_of(e + 6)
                        dve.wait_ge(low.sem, low.upto(m - 1, j))
                    dve.tensor_tensor(xe[:, e % 2, :], SB, xt[:, km % 2, :], ALU.mult).then_inc(xe_sb.sem, 1)

                def low_part(e):
                    dve.wait_ge(xe_hi_sb.sem, xe_hi_sb.upto(n, e + 1))
                    dve.tensor_tensor(xe_lo[:, ring(e), :], xe[:, e % 2, :], xe_hi[:, ring(e), :],
                                      ALU.subtract).then_inc(xe_lo_dve.sem, 1)

                def hidden(m, km, e):
                    dve.wait_ge(g_sb.sem, g_sb.upto(m, e + 1))
                    dve.wait_ge(h3_mm.sem, h3_mm.upto(m, e + 1))
                    if e >= 2:
                        dve.wait_ge(y_mm.sem, y_mm.upto(m, e - 1))
                    elif km > 0:
                        dve.wait_ge(y_mm.sem, y_mm.upto(m - 1, 8 + e))
                    q = (e + km) % 2
                    dve.tensor_tensor(g.f_h[:, q, :], H3[q], g.f_g[:, q, :], ALU.mult).then_inc(h_sb.sem, 1)

                def normalise(m):
                    dve.wait_ge(xt_mm.sem, xt_mm.upto(m - 1))
                    for c in range(4):
                        dve.tensor_scalar(
                            xn[:, c, :], g.x[:, (m * 4 + c).at, :],
                            mean[:, :].rearrange("p (n c) -> p n c", c=4)[:, m.at, c:c + 1],
                            rstd[:, :].rearrange("p (n c) -> p n c", c=4)[:, m.at, c:c + 1],
                            ALU.subtract, ALU.mult).then_inc(xn_sb.sem, 1)

                def best():
                    dve.wait_ge(lg_mm.sem, lg_mm.upto(n + 1))
                    dve.tensor_copy(g.f_lg[:], T[:, 0:4 * E]).then_inc(lg_sb.sem, 1)
                    dve.wait_ge(lg_sb.sem, lg_sb.upto(n + 1))
                    dve.memset(g.s_pad[:, 0:1], 0.0)
                    for t in range(4):
                        ins = dve.max(g.f_top[:, t, :], g.f_lg[:, t * E:(t + 1) * E])
                    ins.then_inc(top_sb.sem, 1)
                    dve.wait_ge(top_sb.sem, top_sb.upto(n + 1))
                    dve.memset(g.s_pad[:, 1:2], 0.0)
                    for t in range(4):
                        ins = dve.max_index(g.f_idx[:, t, :], g.f_top[:, t, :], g.f_lg[:, t * E:(t + 1) * E])
                    ins.then_inc(idx_sb.sem, 1)
                    l3 = g.f_lg[:].rearrange("p (t e) -> p t e", e=E)
                    dve.tensor_tensor(g.f_sh[:].rearrange("p (t e) -> p t e", e=E), l3,
                                                 bc(g.f_top[:, :, 0:1], [P, 4, E]), ALU.subtract).then_inc(sh_sb.sem, 1)
                    dve.wait_ge(idx_sb.sem, idx_sb.upto(n + 1))
                    dve.tensor_copy(g.f_ix[:], g.f_idx[:, :, 0:2]).then_inc(ix_sb.sem, 1)
                    dve.wait_ge(ix_sb.sem, ix_sb.upto(n + 1))
                    for j in range(2):
                        dve.tensor_tensor(g.f_m[:, j, :, :], bc(g.iota[:].unsqueeze(1), [P, 4, E]),
                                                    bc(g.f_ix[:, :, j:j + 1], [P, 4, E]), ALU.is_equal).then_inc(m_sb.sem, 1)
                    dve.wait_ge(m_sb.sem, m_sb.upto(n + 1, 2))
                    dve.tensor_tensor(g.f_m[:, 0, :, :], g.f_m[:, 0, :, :], g.f_m[:, 1, :, :], ALU.add).then_inc(m_sb.sem, 1)

                def gates():
                    dve.wait_ge(pw_sb.sem, pw_sb.upto(n + 1))
                    p3 = g.f_p[:].rearrange("p (t e) -> p t e", e=E)
                    dve.tensor_reduce(g.f_sum[:], p3, AX.X, ALU.add).then_inc(gs_sb.sem, 1)
                    dve.wait_ge(gs_sb.sem, gs_sb.upto(n + 1, 1))
                    dve.reciprocal(g.f_rs[:], g.f_sum[:]).then_inc(gs_sb.sem, 1)
                    dve.wait_ge(m_sb.sem, m_sb.upto(n + 1))
                    dve.tensor_tensor(g.f_m[:, 1, :, :], p3, g.f_m[:, 0, :, :], ALU.mult).then_inc(sc_sb.sem, 1)
                    dve.wait_ge(gs_sb.sem, gs_sb.upto(n + 1))
                    dve.wait_ge(sc_sb.sem, sc_sb.upto(n + 1, 1))
                    dve.tensor_tensor(g.f_m[:, 0, :, :], g.f_m[:, 1, :, :],
                                                 bc(g.f_rs[:].unsqueeze(2), [P, 4, E]), ALU.mult).then_inc(sc_sb.sem, 1)
                    dve.wait_ge(sc_sb.sem, sc_sb.upto(n + 1))
                    dve.wait_ge(st_mm.sem, st_mm.upto(n))
                    dve.tensor_copy(ssp[:, :, 0:E].bitcast(F32R), g.f_m[:, 0, :, :]).then_inc(hi_sb.sem, 1)
                    dve.wait_ge(hi_sb.sem, hi_sb.upto(n + 1))
                    dve.tensor_tensor(ssp[:, :, E:2 * E], g.f_m[:, 0, :, :], ssp[:, :, 0:E], ALU.subtract).then_inc(lo_sb.sem, 1)

                def residual(n, k):
                    dve.wait_ge(y_mm.sem, y_mm.upto(n))
                    dve.tensor_tensor(X4[:, n.at, :], Y[k % 2], X4[:, n.at, :], ALU.add).then_inc(x_sb.sem, 1)
                    if first:
                        dve.wait_ge(x_sb.sem, x_sb.upto(n))
                        dve.wait_ge(rstd_sb.sem, rstd_sb.upto(n - 1))
                        dve.memset(g.s_pad[:, 3:4], 0.0)
                        for c in range(4):
                            ins = dve.bn_stats(g.f_bn[:, c, :], g.x[:, (n * 4 + c).at, :])
                        ins.then_inc(bn_sb.sem, 1)
                        dve.wait_ge(bn_sb.sem, bn_sb.upto(n))
                        dve.memset(g.s_pad[:, 3:4], 0.0)
                        for c in range(4):
                            ins = dve.bn_aggr(g.s_mv[:, c, :], g.f_bn[:, c, :])
                        ins.then_inc(mv_sb.sem, 1)
                        dve.wait_ge(mv_sb.sem, mv_sb.upto(n))
                        dve.tensor_scalar(g.f_vare[:], g.s_mv[:, :, 1], LN_EPS, None, ALU.add).then_inc(vare_sb.sem, 1)
                        dve.tensor_copy(mean_next[:, :].rearrange("p (n c) -> p n c", c=4)[:, n.at, :],
                                        g.s_mv[:, :, 0])

                for e in range(NE):
                    if k == -1 and e == 0:
                        normalise(n + 1)
                    if k + 2 < NCH and e == FF["norm"]:
                        normalise(n + 2)
                    if run and e + 2 in LOW_ON_DVE:
                        low_part(e + 2)
                    for m, km, next_e in ahead(n, k, e, 1):
                        hidden(m, km, next_e)
                    for m, km, next_e in ahead(n, k, e, 3):
                        if next_e < E:
                            scale(m, km, next_e)
                    if gate and e == FF["best"]:
                        best()
                    if gate and e == FF["gates"]:
                        gates()
                    if 0 <= k - 1 < NCH and e == FF["residual"]:
                        residual(n - 1, k - 1)

            march(dve, body)

        if not first:
            @block.sync
            def _(sp):
                view = out.rearrange("(n s) (c p) d -> n p (s c) d", s=2, p=P)
                with sp.Fori(0, NCH) as n:
                    sp.wait_ge(x_sb.sem, x_sb.upto(Step(n, 1, 0)))
                    sp.dma_start(view[n], g.x[:, :, :].rearrange("p (n c) d -> p n c d", c=4)[:, n, :, :]
                                 ).then_inc(stored, 16)
                sp.wait_ge(stored, 16 * NCH)


def program(nc, d, out):
    with ExitStack() as ctx:
        g = Shared()

        def sb(name, shape, dt=F32):
            return ctx.enter_context(nc.sbuf_tensor(name, shape, dt))

        g.x = sb("x", [P, NT, DIM])
        g.mean = [sb(f"mean{i}", [P, NT]) for i in range(4)]
        g.s_mv = sb("s_mv", [P, 4, 2])
        g.rstd = [sb(f"rstd{i}", [P, NT]) for i in range(4)]
        g.identity = sb("identity", [P, P])
        g.wqkv_a, g.wqkv_b = sb("wqkv_a", [P, 3 * P]), sb("wqkv_b", [P, 3 * P])
        g.bqkv, g.bproj = sb("bqkv", [P, 3 * P]), sb("bproj", [P, DIM])
        g.qk_w, g.qk_scale = sb("qk_w", [P, 2, HD]), sb("qk_scale", [P, DIM])
        g.minus_bound, g.minus_lam = sb("minus_bound", [P, 1]), sb("minus_lam", [P, 1])
        g.wproj, g.wo = sb("wproj", [P, DIM]), sb("wo", [P, DIM])
        g.lam_in = sb("lam_in", [P, 4, HD])
        g.select_raw, g.select = sb("select_raw", [P, E, P]), sb("select", [P, E, P], F32R)
        g.iota, g.gate = sb("iota", [P, E]), sb("gate", [P, E])
        g.w1, g.w3, g.w2 = (sb(x, [P, E + 1, P]) for x in ("w1", "w3", "w2"))
        g.w1_hi, g.w1_lo, g.w3_hi, g.w3_lo = (sb(x, [P, E + 1, P], F32R) for x in ("w1_hi", "w1_lo", "w3_hi", "w3_lo"))
        g.rope_cos, g.rope_sin = sb("rope_cos", [P, 512]), sb("rope_sin", [P, 512])
        g.minus_half, g.three_halves = sb("minus_half", [P, 16]), sb("three_halves", [P, 64])
        g.euler = sb("euler", [P, 4 * E])
        g.s_xn, g.s_xt = sb("s_xn", [P, 2, 2, DIM]), sb("s_xt", [P, SEQ])
        g.s_qkv, g.s_qh = sb("s_qkv", [P, 2, 3, 2, P]), sb("s_qh", [P, 2, 256])
        g.s_qs, g.s_ks = sb("s_qs", [P, 2, 2, 512]), sb("s_ks", [P, 2, 2, 512])
        g.s_v1 = sb("s_v1", [P, 2, 2, HEADS, 32])
        g.s_kt, g.s_qt = sb("s_kt", [P, 2, 4, SEQ], F32R), sb("s_qt", [P, 2, 4, SEQ], F32R)
        g.s_qp = sb("s_qp", [P, 4, SEQ], F32R)
        g.s_probs = sb("s_probs", [P, 8, 2, SEQ])
        g.s_ot, g.s_an, g.s_at = sb("s_ot", [P, 2, 4, SEQ]), sb("s_an", [P, 2, DIM]), sb("s_at", [P, SEQ])
        g.s_sq, g.s_ss, g.s_vh = sb("s_sq", [P, 512]), sb("s_ss", [P, 64]), sb("s_vh", [P, 64])
        g.s_v, g.s_i, g.s_y, g.s_yt = sb("s_v", [P, 64]), sb("s_i", [P, 64], I32), sb("s_y", [P, 64]), sb("s_yt", [P, 64])
        g.s_rs, g.s_tv, g.s_a2 = sb("s_rs", [P, HEADS]), sb("s_tv", [P, 256]), sb("s_a2", [P, 2, DIM])
        g.s_rot, g.s_pad = sb("s_rot", [P, 2, 512]), sb("s_pad", [P, 4])
        g.s_sq2, g.s_ms2, g.s_var2, g.s_inv2 = (sb(x, [P, w]) for x, w in (
            ("s_sq2", 256), ("s_ms2", 16), ("s_var2", 16), ("s_inv2", 16)))
        g.s_bn, g.s_vare = sb("s_bn", [P, 2, 6]), sb("s_vare", [P, 2])
        g.f_xn, g.f_xt = sb("f_xn", [P, 4, DIM]), sb("f_xt", [P, 2, CH])
        g.f_ss, g.f_st = sb("f_ss", [P, 4, P]), sb("f_st", [P, 2, CH], F32R)
        g.f_xe, g.f_g, g.f_h = (sb(x, [P, 2, CH]) for x in ("f_xe", "f_g", "f_h"))
        g.f_xe_hi, g.f_xe_lo = sb("f_xe_hi", [P, 5, CH], F32R), sb("f_xe_lo", [P, 5, CH], F32R)
        g.f_lg, g.f_sh, g.f_p = (sb(x, [P, 4 * E]) for x in ("f_lg", "f_sh", "f_p"))
        g.f_top, g.f_idx, g.f_ix = sb("f_top", [P, 4, E]), sb("f_idx", [P, 4, E], U32), sb("f_ix", [P, 4, 2])
        g.f_m, g.f_sum, g.f_rs = sb("f_m", [P, 2, 4, E]), sb("f_sum", [P, 4]), sb("f_rs", [P, 4])
        g.f_bn, g.f_vare = sb("f_bn", [P, 4, 6]), sb("f_vare", [P, 4])
        psum = ctx.enter_context(nc.psum_tensor("psum", [P, 4096], F32))

        setup(nc, ctx, g, d)
        attention(nc, ctx, g, "a", psum)
        feed_forward(nc, ctx, g, "f", psum, None)
        attention(nc, ctx, g, "b", psum)
        feed_forward(nc, ctx, g, "h", psum, out)


def constants():
    identity = np.eye(P, dtype=np.float32)
    select = np.zeros((P, E, P), np.float32)
    for e in range(E):
        select[e, e, :] = 1.0
        select[E + e, e, :] = 1.0
    iota = np.tile(np.arange(E, dtype=np.float32), (P, 1))
    inv_freq = 1.0 / 10000.0 ** (np.arange(0, HD, 2, dtype=np.float64) / HD)
    pos = np.arange(SEQ, dtype=np.float64)
    freqs = np.repeat(np.float32(pos[:, None]) * np.float32(inv_freq[None, :]), 2, axis=-1).astype(np.float64)
    sv = (np.arange(0, HD, 2, dtype=np.float64) + 0.4 * HD) / (1.4 * HD)
    scale = sv[None, :] ** ((pos - SEQ // 2) / 512.0)[:, None]
    scale = np.concatenate([scale, scale], axis=-1)
    sign = np.where(np.arange(HD) % 2 == 0, -1.0, 1.0)

    def table(f):
        both = np.stack([f * scale * HD ** -0.5, f / scale])
        both = np.tile(both.reshape(2, 2, P, 1, HD), (1, 1, 1, HEADS, 1))
        return np.ascontiguousarray(both.transpose(2, 0, 1, 3, 4).reshape(P, 512).astype(np.float32))

    return {"identity": identity, "select": select, "iota": iota,
            "rope_cos": table(np.cos(freqs)), "rope_sin": table(np.sin(freqs) * sign)}


def kernel(**inputs):
    import concourse.bacc as bacc
    from concourse.bass_utils import run_bass_kernel_spmd

    def get(name):
        return np.asarray(inputs[name])

    arrays = {"x": get("L0_attn_a_x"),
              "Wqkv_aT": get("L0_attn_a_Wqkv").T, "WprojT": get("L0_attn_a_Wproj").T,
              "bqkv": get("L0_attn_a_bqkv"), "bproj": get("L0_attn_a_bproj"),
              "qn_w": get("L0_attn_a_qn_w"), "kn_w": get("L0_attn_a_kn_w"),
              "Wqkv_bT": np.concatenate([get(f"L0_attn_b_{w}").T for w in ("Wq", "Wk", "Wv")], axis=1),
              "WoT": get("L0_attn_b_Wo").T,
              "gate_wT": get("L0_ffn_gate_w").T}
    for w in ("lambda_q1", "lambda_k1", "lambda_q2", "lambda_k2"):
        arrays[w] = get(f"L0_attn_b_{w}")
    for w in ("w1", "w2", "w3", "w1s", "w2s", "w3s"):
        arrays[w] = get(f"L0_ffn_{w}")
    arrays.update(constants())

    nc = bacc.Bacc("TRN2", target_bir_lowering=False, num_devices=1)
    given, d = {}, {}
    for name, array in arrays.items():
        array = np.ascontiguousarray(array)
        given[f"in_{name}"] = array
        d[name] = nc.dram_tensor(f"in_{name}", array.shape, mybir.dt.from_np(array.dtype), kind="ExternalInput").ap()
    out = nc.dram_tensor("out_0", (NSEQ, SEQ, DIM), F32, kind="ExternalOutput").ap()
    program(nc, d, out)
    result = run_bass_kernel_spmd(nc, [given], core_ids=[0])
    return result.results[0]["out_0"]
```
